# Optimizing a Trainium2 kernel written in Bass

```python
import numpy as np
import jax
import jax.numpy as jnp

def _softmax(x, axis=-1):
    return jax.nn.softmax(x, axis=axis)

def _gelu(x):
    return jax.nn.gelu(x, approximate=True)

def _silu(x):
    return jax.nn.silu(x)

def _sigmoid(x):
    return jax.nn.sigmoid(x)

def _layernorm(x, axis=-1, eps=1e-05):
    m = jnp.mean(x, axis=axis, keepdims=True)
    v = jnp.var(x, axis=axis, keepdims=True)
    return (x - m) / jnp.sqrt(v + eps)

def _scatter_add(tgt, idx, src, axis=0):
    return tgt.at[idx].add(src)

def _segment_sum(src, seg, n):
    return jax.ops.segment_sum(src, seg, n)
kernel_name = 'mk_xattn_ffn_d2_seqx_r8_b82d88'

def setup_inputs(seed: int=0):
    np.random.seed(seed)
    _w = jnp.asarray

    def _rec_inputs():
        import jax
        import jax.numpy as jnp
        _rk = jax.random.key(seed)
        x = 0.002226 + 0.9996 * jax.random.normal(jax.random.fold_in(_rk, 1), (1, 1024, 128), jnp.float32)
        _lenS = 1024 - jax.random.randint(jax.random.fold_in(_rk, 7), (1,), 0, max(1, 1024 // 4) + 1, jnp.int32)
        _lenS2 = 6404 - jax.random.randint(jax.random.fold_in(_rk, 8), (1,), 0, max(1, 6404 // 4) + 1, jnp.int32)
        _ctx_1024P = jax.random.normal(jax.random.fold_in(_rk, 11), (1, 16, 128), jnp.float32)
        _ctx_1024c = jax.random.dirichlet(jax.random.fold_in(_rk, 511), 0.3 * jnp.ones((16,), jnp.float32), (1, 6404))
        _ctx_1024t = jnp.einsum('bsk,bkd->bsd', _ctx_1024c, _ctx_1024P)
        _ctx_1024t = _ctx_1024t * jax.lax.rsqrt(jnp.mean(jnp.square(_ctx_1024t)) + 1e-12) * 0.953939
        ctx_1024 = -0.000125008 + 0.999885 * (_ctx_1024t + 0.3 * jax.random.normal(jax.random.fold_in(_rk, 611), (1, 6404, 128), jnp.float32))
        return (x, ctx_1024)
    x, ctx_1024 = _rec_inputs()

    def _L0_xattn_setup():
        import jax, jax.numpy as jnp
        import numpy as np
        EPS = 1e-05

        def layer_norm(x, g, b):
            mu = jnp.mean(x, axis=-1, keepdims=True)
            var = jnp.var(x, axis=-1, keepdims=True)
            return (x - mu) * jax.lax.rsqrt(var + EPS) * g + b
        key = jax.random.key(seed)
        ks = jax.random.split(key, 8)
        dim, heads, dim_head = (128, 16, 64)
        inner = heads * dim_head
        b, n, m = (8, 512, 64)
        s = dim ** (-0.5)
        return {'x': jax.random.normal(ks[0], (b, n, dim), jnp.float32), 'latents': jax.random.normal(ks[1], (b, m, dim), jnp.float32), 'ln_m_g': jnp.ones((dim,), jnp.float32), 'ln_m_b': jnp.zeros((dim,), jnp.float32), 'ln_l_g': jnp.ones((dim,), jnp.float32), 'ln_l_b': jnp.zeros((dim,), jnp.float32), 'Wq': jax.random.normal(ks[2], (dim, inner), jnp.float32) * s, 'Wkv': jax.random.normal(ks[3], (dim, 2 * inner), jnp.float32) * s, 'Wout': jax.random.normal(ks[4], (inner, dim), jnp.float32) * s}
    _L0_xattn_all = _L0_xattn_setup()
    _L0_xattn_in = {k: v for k, v in _L0_xattn_all.items() if k in ('ln_m_g', 'ln_m_b', 'ln_l_g', 'ln_l_b', 'Wq', 'Wkv', 'Wout')}
    del _L0_xattn_all

    def _L0_ffn_setup():
        import jax, jax.numpy as jnp
        import numpy as np
        DM = 128
        NEXPERTS = 32
        EXPERTSETS = 4
        EXPERTSIZE = 32
        BATCH, SEQ = (4, 256)
        key = jax.random.key(seed)
        k0, k1, k2, k3 = jax.random.split(key, 4)
        scale = 0.02
        x = jax.random.normal(k0, (BATCH, SEQ, DM), jnp.float32)
        controller = jax.random.normal(k1, (DM, NEXPERTS, EXPERTSETS), jnp.float32) * scale
        f1 = jax.random.normal(k2, (DM, NEXPERTS, EXPERTSETS, EXPERTSIZE), jnp.float32) * scale
        bias = jnp.zeros((NEXPERTS, EXPERTSETS, EXPERTSIZE), jnp.float32)
        f2 = jax.random.normal(k3, (NEXPERTS, EXPERTSETS, EXPERTSIZE, DM), jnp.float32) * scale
        return {'x': x, 'controller': controller, 'f1': f1, 'bias': bias, 'f2': f2}
    _L0_ffn_all = _L0_ffn_setup()
    _L0_ffn_in = {k: v for k, v in _L0_ffn_all.items() if k in ('controller', 'f1', 'bias', 'f2')}
    del _L0_ffn_all

    def _L1_xattn_setup():
        import jax, jax.numpy as jnp
        import numpy as np
        B, C_LEN, Q_LEN, D = (8, 256, 64, 128)
        key = jax.random.key(seed)
        ks = jax.random.split(key, 10)
        scale = 1.0 / np.sqrt(D)
        return {'c': jax.random.normal(ks[0], (B, C_LEN, D), dtype=jnp.float32), 'q': jax.random.normal(ks[1], (B, Q_LEN, D), dtype=jnp.float32), 'w_cq': jax.random.normal(ks[2], (D,), dtype=jnp.float32) * scale, 'b_cq': jax.random.normal(ks[3], (), dtype=jnp.float32) * scale, 'w_c': jax.random.normal(ks[4], (D,), dtype=jnp.float32) * scale, 'b_c': jax.random.normal(ks[5], (), dtype=jnp.float32) * scale, 'w_q': jax.random.normal(ks[6], (D,), dtype=jnp.float32) * scale, 'b_q': jax.random.normal(ks[7], (), dtype=jnp.float32) * scale, 'W_l': jax.random.normal(ks[8], (D, 4 * D), dtype=jnp.float32) * (1.0 / np.sqrt(4 * D)), 'b_l': jax.random.normal(ks[9], (D,), dtype=jnp.float32) * (1.0 / np.sqrt(4 * D))}
    _L1_xattn_all = _L1_xattn_setup()
    _L1_xattn_in = {k: v for k, v in _L1_xattn_all.items() if k in ('w_cq', 'b_cq', 'w_c', 'b_c', 'w_q', 'b_q', 'W_l', 'b_l')}
    del _L1_xattn_all

    def _L1_ffn_setup():
        import jax, jax.numpy as jnp
        import numpy as np
        DM, NEXPERTS, SETS, ESIZE = (128, 32, 4, 32)
        B, S = (2, 1024)
        key = jax.random.key(seed)
        ks = jax.random.split(key, 7)
        sc = 0.02
        return {'x': jax.random.normal(ks[0], (B, S, DM), jnp.float32), 'Wc': jax.random.normal(ks[1], (DM, NEXPERTS, SETS), jnp.float32) * sc, 'bc': jax.random.normal(ks[2], (NEXPERTS, SETS), jnp.float32) * sc, 'W1': jax.random.normal(ks[3], (NEXPERTS, SETS, DM, ESIZE), jnp.float32) * sc, 'b1': jax.random.normal(ks[4], (NEXPERTS, SETS, ESIZE), jnp.float32) * sc, 'W2': jax.random.normal(ks[5], (NEXPERTS, SETS, DM, ESIZE), jnp.float32) * sc, 'b2': jax.random.normal(ks[6], (NEXPERTS, SETS, DM), jnp.float32) * sc}
    _L1_ffn_all = _L1_ffn_setup()
    _L1_ffn_in = {k: v for k, v in _L1_ffn_all.items() if k in ('Wc', 'bc', 'W1', 'b1', 'W2', 'b2')}
    del _L1_ffn_all
    return {'x': x, 'ctx_1024': ctx_1024, 'L0_xattn_ln_m_g': _L0_xattn_in['ln_m_g'], 'L0_xattn_ln_m_b': _L0_xattn_in['ln_m_b'], 'L0_xattn_ln_l_g': _L0_xattn_in['ln_l_g'], 'L0_xattn_ln_l_b': _L0_xattn_in['ln_l_b'], 'L0_xattn_Wq': _L0_xattn_in['Wq'], 'L0_xattn_Wkv': _L0_xattn_in['Wkv'], 'L0_xattn_Wout': _L0_xattn_in['Wout'], 'L0_ffn_controller': _L0_ffn_in['controller'], 'L0_ffn_f1': _L0_ffn_in['f1'], 'L0_ffn_bias': _L0_ffn_in['bias'], 'L0_ffn_f2': _L0_ffn_in['f2'], 'L1_xattn_w_cq': _L1_xattn_in['w_cq'], 'L1_xattn_b_cq': _L1_xattn_in['b_cq'], 'L1_xattn_w_c': _L1_xattn_in['w_c'], 'L1_xattn_b_c': _L1_xattn_in['b_c'], 'L1_xattn_w_q': _L1_xattn_in['w_q'], 'L1_xattn_b_q': _L1_xattn_in['b_q'], 'L1_xattn_W_l': _L1_xattn_in['W_l'], 'L1_xattn_b_l': _L1_xattn_in['b_l'], 'L1_ffn_Wc': _L1_ffn_in['Wc'], 'L1_ffn_bc': _L1_ffn_in['bc'], 'L1_ffn_W1': _L1_ffn_in['W1'], 'L1_ffn_b1': _L1_ffn_in['b1'], 'L1_ffn_W2': _L1_ffn_in['W2'], 'L1_ffn_b2': _L1_ffn_in['b2']}

def reference(x, ctx_1024, L0_xattn_ln_m_g, L0_xattn_ln_m_b, L0_xattn_ln_l_g, L0_xattn_ln_l_b, L0_xattn_Wq, L0_xattn_Wkv, L0_xattn_Wout, L0_ffn_controller, L0_ffn_f1, L0_ffn_bias, L0_ffn_f2, L1_xattn_w_cq, L1_xattn_b_cq, L1_xattn_w_c, L1_xattn_b_c, L1_xattn_w_q, L1_xattn_b_q, L1_xattn_W_l, L1_xattn_b_l, L1_ffn_Wc, L1_ffn_bc, L1_ffn_W1, L1_ffn_b1, L1_ffn_W2, L1_ffn_b2):
    import jax
    import jax.numpy as jnp

    def _L0_xattn_ref(x, latents, ln_m_g, ln_m_b, ln_l_g, ln_l_b, Wq, Wkv, Wout):
        import jax, jax.numpy as jnp
        import numpy as np
        EPS = 1e-05

        def layer_norm(x, g, b):
            mu = jnp.mean(x, axis=-1, keepdims=True)
            var = jnp.var(x, axis=-1, keepdims=True)
            return (x - mu) * jax.lax.rsqrt(var + EPS) * g + b
        heads, dim_head = (16, 64)
        scale = dim_head ** (-0.5)
        x = layer_norm(x, ln_m_g, ln_m_b)
        lat = layer_norm(latents, ln_l_g, ln_l_b)
        b, m, _ = lat.shape
        q = lat @ Wq
        kv_input = jnp.concatenate([x, lat], axis=1)
        kv = kv_input @ Wkv
        k, v = jnp.split(kv, 2, axis=-1)

        def split_heads(t):
            return t.reshape(t.shape[0], t.shape[1], heads, dim_head).transpose(0, 2, 1, 3)
        q, k, v = (split_heads(q), split_heads(k), split_heads(v))
        dots = jnp.einsum('bhid,bhjd->bhij', q, k) * scale
        attn = jax.nn.softmax(dots, axis=-1)
        out = jnp.einsum('bhij,bhjd->bhid', attn, v)
        out = out.transpose(0, 2, 1, 3).reshape(b, m, heads * dim_head)
        return out @ Wout

    def _L0_ffn_ref(x, controller, f1, bias, f2):
        import jax, jax.numpy as jnp
        import numpy as np
        DM = 128
        NEXPERTS = 32
        EXPERTSETS = 4
        EXPERTSIZE = 32
        BATCH, SEQ = (4, 256)
        B, L, d = x.shape
        t = controller.shape[1]
        g = L // t
        grouped = x.reshape(B, g, t, d)
        logits = jnp.einsum('bgtd,des->bgtes', grouped, controller)
        tie = jnp.linspace(0.0, 1e-06, t, dtype=logits.dtype).reshape(t, 1, 1)
        logits = logits + tie
        perm = (logits == jnp.max(logits, axis=-3, keepdims=True)).astype(x.dtype)
        perm = jax.lax.stop_gradient(perm)
        dispatched = jnp.einsum('bgtd,bgtes->bgesd', grouped, perm)
        inner = jax.nn.relu(jnp.einsum('bgesd,desf->bgesf', dispatched, f1) + bias)
        intermediate = jnp.einsum('bgesf,esfd->bgesd', inner, f2)
        out = jnp.einsum('bgesd,bgtes->bgtd', intermediate, perm)
        return out.reshape(B, L, d)

    def _L1_xattn_ref(c, q, w_cq, b_cq, w_c, b_c, w_q, b_q, W_l, b_l):
        import jax, jax.numpy as jnp
        import numpy as np
        B, C_LEN, Q_LEN, D = (8, 256, 64, 128)
        cq = jnp.einsum('bcd,bqd,d->bcq', c, q, w_cq) + b_cq
        s = (c @ w_c + b_c)[:, :, None] + (q @ w_q + b_q)[:, None, :] + cq
        a = jax.nn.softmax(s, axis=2)
        c2q_att = jnp.einsum('bcq,bqd->bcd', a, q)
        b_att = jax.nn.softmax(jnp.max(s, axis=2), axis=1)
        q2c_att = jnp.einsum('bc,bcd->bd', b_att, c)[:, None, :]
        x = jnp.concatenate([c, c2q_att, c * c2q_att, c * q2c_att], axis=-1)
        z = x @ W_l.T + b_l
        return z

    def _L1_ffn_ref(x, Wc, bc, W1, b1, W2, b2):
        import jax, jax.numpy as jnp
        import numpy as np
        DM, NEXPERTS, SETS, ESIZE = (128, 32, 4, 32)
        B, S = (2, 1024)
        b, s, d = x.shape
        g = Wc.shape[1]
        grouped = x.reshape(b, s // g, g, d)
        logits = jnp.einsum('bntd,des->bntes', grouped, Wc) + bc
        tie = jnp.linspace(0.0, 1e-06, g, dtype=x.dtype).reshape(-1, 1, 1)
        logits = logits + tie
        perm = (logits == jnp.max(logits, axis=-3, keepdims=True)).astype(x.dtype)
        permuted = jnp.einsum('bntd,bntes->bnesd', grouped, perm)
        inner = jax.nn.relu(jnp.einsum('bnesd,esdf->bnesf', permuted, W1) + b1)
        result_permuted = jnp.einsum('bnesf,esdf->bnesd', inner, W2) + b2
        result = jnp.einsum('bnesd,bntes->bntd', result_permuted, perm)
        return result.reshape(b, s, d)
    x = x + _L0_xattn_ref(ctx_1024, _layernorm(x, axis=-1), L0_xattn_ln_m_g, L0_xattn_ln_m_b, L0_xattn_ln_l_g, L0_xattn_ln_l_b, L0_xattn_Wq, L0_xattn_Wkv, L0_xattn_Wout)
    x = x + _L0_ffn_ref(_layernorm(x, axis=-1), L0_ffn_controller, L0_ffn_f1, L0_ffn_bias, L0_ffn_f2)
    x = x + _L1_xattn_ref(_layernorm(x, axis=-1), ctx_1024, L1_xattn_w_cq, L1_xattn_b_cq, L1_xattn_w_c, L1_xattn_b_c, L1_xattn_w_q, L1_xattn_b_q, L1_xattn_W_l, L1_xattn_b_l)
    x = x + _L1_ffn_ref(_layernorm(x, axis=-1), L1_ffn_Wc, L1_ffn_bc, L1_ffn_W1, L1_ffn_b1, L1_ffn_W2, L1_ffn_b2)
    return x

_drawn_inputs = setup_inputs


def setup_inputs(seed=0):
    import zlib

    import numpy as np

    out = dict(_drawn_inputs(seed))
    spreads = {'L0_xattn_ln_m_g': (1.0, 0.2),
     'L0_xattn_ln_m_b': (0.0, 0.1),
     'L0_xattn_ln_l_g': (1.0, 0.2),
     'L0_xattn_ln_l_b': (0.0, 0.1),
     'L0_ffn_bias': (0.0, 0.8)}
    factors = {'L0_ffn_f1': 3.155,
     'L1_xattn_w_c': 4.903,
     'L1_ffn_W1': 3.681,
     'L1_ffn_b1': 8.0,
     'L1_ffn_W2': 3.024,
     'L1_ffn_b2': 2.793}
    for name, (base, spread) in spreads.items():
        noise = np.random.default_rng([zlib.crc32(name.encode()), seed]).standard_normal(out[name].shape)
        drawn = base * np.exp(spread * noise) if base else spread * noise
        out[name] = jnp.asarray(drawn.astype(out[name].dtype))
    for name, factor in factors.items():
        out[name] = (out[name] * factor).astype(out[name].dtype)
    return out
```

```python
from contextlib import ExitStack

import concourse.bass as bass
from concourse import mybir

F32 = mybir.dt.float32
F16 = mybir.dt.float16
BF16 = mybir.dt.bfloat16
ALU = mybir.AluOpType
ACT = mybir.ActivationFunctionType
AX = mybir.AxisListType

P = 128
TOKENS, CONTEXT, D = 1024, 6404, 128
TOKEN_TILES = TOKENS // P
CTX_TILES = CONTEXT // P
CTX_ROWS = CTX_TILES * P
TAIL = CONTEXT - CTX_ROWS
EPS = 1e-5

HEADS, DH = 16, 64
KEYS = CONTEXT + TOKENS
FULL_TILES = CTX_TILES + TOKEN_TILES
KEY_TILES = FULL_TILES + 1
KEY_COLS = KEY_TILES * P
LATENT_COL = CTX_TILES * P
BANK = 512
K_CHUNKS = -(-KEYS // BANK)
V_GROUPS = -(-KEY_TILES // 8)
VCOLS = 2 * DH + 1
BODY = 14
BODIES = FULL_TILES // BODY
LOOP_TILES = BODY * BODIES
MAX_CHUNKS = 7
MAX_SLOTS = TOKEN_TILES * MAX_CHUNKS
REST_COL = MAX_CHUNKS * 2 * BANK
REST = KEYS - REST_COL
REST_STEPS = TOKEN_TILES // 2
SCALE = DH ** -0.5
LIFT = 6.931471805599453 / SCALE

EXPERTS, SETS, ESIZE = 32, 4, 32
ES = EXPERTS * SETS
GROUP = EXPERTS
GROUPS = TOKENS // GROUP
TIE_STEP = 1e-6 / (GROUP - 1)


class Steps:

    def __init__(self, engine, sem):
        self.engine, self.sem, self.count = engine, sem, 0

    def done(self, instruction):
        instruction.then_inc(self.sem, 1)
        self.count += 1

    def link(self, instruction):
        self.done(instruction)
        self.engine.wait_ge(self.sem, self.count)


class Scope(ExitStack):

    def __init__(self, nc, name, whole=None):
        super().__init__()
        self.nc, self.name = nc, name
        self.semaphores = whole.semaphores if whole else []

    def sb(self, name, shape, dtype=F32):
        return self.enter_context(self.nc.sbuf_tensor(f"{self.name}_{name}", shape, dtype))

    def ps(self, name, shape, dtype=F32):
        return self.enter_context(self.nc.psum_tensor(f"{self.name}_{name}", shape, dtype))

    def sem(self, name):
        sem = self.nc.alloc_semaphore(name=f"{self.name}_{name}")
        self.semaphores.append(sem)
        return sem

    def clear_semaphores(self):
        self.nc.all_engine_barrier()
        self.nc.clear_and_free_semaphores(self.semaphores)
        self.nc.all_engine_barrier()
        self.semaphores.clear()


class NormState:

    def __init__(self, sc, name, tiles):
        self.stats = sc.sb(name + "_stats", [P, tiles, 6])
        self.a = sc.sb(name + "_a", [P, tiles])
        self.b = sc.sb(name + "_b", [P, tiles])
        self.var = sc.sb(name + "_var", [P, tiles])
        self.mean = sc.sb(name + "_mean", [P, tiles])
        self.std = sc.sb(name + "_std", [P, tiles])
        self.rstd = sc.sb(name + "_rstd", [P, tiles])
        self.var_ready = sc.sem(name + "_var_ready")
        self.std_ready = sc.sem(name + "_std_ready")


def norm_moments(dve, steps, ns, lo, hi, n=P):
    st = ns.stats
    a, b, var, mean = (t[0:n, lo:hi] for t in (ns.a, ns.b, ns.var, ns.mean))
    steps.done(dve.tensor_tensor(a, st[0:n, lo:hi, 1], st[0:n, lo:hi, 4], op=ALU.add))
    steps.done(dve.tensor_tensor(b, st[0:n, lo:hi, 1], st[0:n, lo:hi, 4], op=ALU.subtract))
    steps.link(dve.tensor_tensor(var, st[0:n, lo:hi, 2], st[0:n, lo:hi, 5], op=ALU.add))
    steps.done(dve.tensor_scalar(mean, a, 0.5, None, ALU.mult))
    steps.done(dve.tensor_scalar(var, var, 1.0 / D, EPS, ALU.mult, ALU.add))
    steps.link(dve.tensor_tensor(b, b, b, op=ALU.mult))
    dve.scalar_tensor_tensor(var, b, 0.25, var, ALU.mult, ALU.add).then_inc(ns.var_ready, 1)


def norm_rstd(dve, steps, ns, lo, hi, turn, n=P):
    var, std, r, a = (t[0:n, lo:hi] for t in (ns.var, ns.std, ns.rstd, ns.a))
    dve.wait_ge(ns.std_ready, turn)
    steps.link(dve.reciprocal(r, std))
    steps.link(dve.tensor_tensor(a, r, r, op=ALU.mult))
    steps.link(dve.tensor_tensor(a, a, var, op=ALU.mult))
    steps.link(dve.tensor_scalar(a, a, -0.5, 1.5, ALU.mult, ALU.add))
    steps.link(dve.tensor_tensor(r, r, a, op=ALU.mult))


def norm_sqrt(act, ns, lo, hi, turn, n=P):
    act.wait_ge(ns.var_ready, turn)
    act.activation(ns.std[0:n, lo:hi], ns.var[0:n, lo:hi], ACT.Sqrt).then_inc(ns.std_ready, 1)


def normalize(dve, out, in_, ns, t, n=P):
    return dve.tensor_scalar(out, in_, ns.mean[0:n, t:t + 1], ns.rstd[0:n, t:t + 1], ALU.subtract, ALU.mult)


def column(vector):
    return vector.rearrange("(p one) -> p one", one=1)


def spread_columns(a, n):
    return a.rearrange("p (k one) -> p k one", one=1).to_broadcast([a.shape[0], a.shape[1], n])


def row(vector):
    return vector.rearrange("(one n) -> one n", one=1)


def stage_prepare(nc, pers, A):
    sc = Scope(nc, "prep", pers.whole)
    with sc:
        ctx = sc.sb("ctx", [P, CTX_TILES, D])
        tail = sc.sb("tail", [TAIL, D])
        lat = sc.sb("lat", [P, TOKEN_TILES, D])
        wq = sc.sb("wq", [P, HEADS * DH])
        wkv = sc.sb("wkv", [P, 2 * HEADS * DH])
        gains = sc.sb("gains", [P, 4])
        NF = 4
        full = sc.sb("full", [P, NF, BANK])
        T = [pers.banks[:, n, :] for n in range(NF)]
        nx = NormState(sc, "nx", TOKEN_TILES)
        nl = NormState(sc, "nl", TOKEN_TILES)
        nk = NormState(sc, "nk", CTX_TILES + 1)
        x_in, w_in, g_in, tail_in = (sc.sem(n) for n in ("x_in", "w_in", "g_in", "tail_in"))
        CL = 5
        PER = CTX_TILES // CL
        ctx_in = [sc.sem(f"ctx_in{n}") for n in range(CL)]
        zeroed, ident_ready = sc.sem("zeroed"), sc.sem("ident_ready")
        vec, tile_ready, transposed = sc.sem("vec"), sc.sem("tile_ready"), sc.sem("transposed")
        full_ready, high_ready, low_ready = sc.sem("full_ready"), sc.sem("high_ready"), sc.sem("low_ready")
        w_high = sc.sem("w_high")
        w_done = sc.sem("w_done")
        X, kvh, kvl, ident = pers.X, pers.kvh, pers.kvl, pers.ident

        def tiles_of(c):
            return [t for t in range(4 * c, min(4 * c + 4, KEY_TILES))]

        def width(c):
            return min(BANK, KEYS - c * BANK)

        block = sc.enter_context(nc.Block())

        @block.sync
        def _(sp):
            sp.dma_start(X[:, :, :], A["x"][0].rearrange("(t p) d -> p t d", p=P)).then_inc(x_in, 16)
            body = A["ctx"][0, 0:CTX_ROWS, :].rearrange("(p t) d -> p t d", p=P)
            for n in range(CL):
                sp.dma_start(ctx[:, n * PER:(n + 1) * PER, :], body[:, n * PER:(n + 1) * PER, :])\
                  .then_inc(ctx_in[n], 16)
            sp.dma_start(tail[:, :], A["ctx"][0, CTX_ROWS:CONTEXT, :]).then_inc(tail_in, 16)

        @block.scalar
        def _(act):
            for n, v in enumerate((A["ln_m_g"], A["ln_m_b"], A["ln_l_g"], A["ln_l_b"])):
                act.dma_start(gains[:, n:n + 1], column(v)).then_inc(g_in, 16)
            act.dma_start(wkv[:, :], A["wkv"]).then_inc(w_in, 16)
            act.dma_start(wq[:, :], A["wq"]).then_inc(w_in, 16)
            norm_sqrt(act, nx, 0, TOKEN_TILES, 1)
            norm_sqrt(act, nl, 0, TOKEN_TILES, 1)
            for n in range(CL):
                norm_sqrt(act, nk, n * PER, (n + 1) * PER, n + 1)
            norm_sqrt(act, nk, CTX_TILES, CTX_TILES + 1, CL + 1, TAIL)
            act.wait_ge(w_in, 32)
            for r in range(2):
                act.activation(pers.wk_h[:, :, r, :], wkv[:, 0:1024].rearrange("p (h d) -> p h d", d=DH), ACT.Copy)\
                   .then_inc(w_high, 1)
                act.activation(pers.wq_h[:, :, r, :], wq[:, :].rearrange("p (h d) -> p h d", d=DH), ACT.Copy)\
                   .then_inc(w_high, 1)
            act.activation(pers.wv_h[:, :], wkv[:, 1024:2048], ACT.Copy).then_inc(w_high, 1)
            act.wait_ge(g_in, 64)
            for c in range(K_CHUNKS):
                act.wait_ge(transposed, c + 1)
                if c >= NF:
                    act.wait_ge(low_ready, c - NF + 1)
                w = width(c)
                parts = []
                for t in tiles_of(c):
                    n = TAIL if t == FULL_TILES else P
                    kind = 2 if CTX_TILES <= t < FULL_TILES else 0
                    o = (t % 4) * P
                    if parts and parts[-1][2] == kind:
                        parts[-1][1] = o + n
                    else:
                        parts.append([o, o + n, kind])
                for o0, o1, kind in parts:
                    g, b = gains[:, kind:kind + 1], gains[:, kind + 1:kind + 2]
                    last = act.activation(full[:, c % NF, o0:o1], T[c % NF][:, o0:o1], ACT.Identity, bias=b, scale=g)
                    if o1 == w:
                        last.then_inc(full_ready, 1)
                    last = act.activation(kvh[:, c * BANK + o0:c * BANK + o1], T[c % NF][:, o0:o1], ACT.Identity,
                                          bias=b, scale=g)
                    if o1 == w:
                        last.then_inc(high_ready, 1)

        @block.gpsimd
        def _(pool):
            pool.memset(ident[:, :], 0.0).then_inc(zeroed, 1)
            pool.wait_ge(zeroed, 1)
            pool.affine_select(out=ident[:, :], in_=ident[:, :], compare_op=ALU.not_equal, fill=1.0, base=0,
                               pattern=[[-1, P]], channel_multiplier=1).then_inc(ident_ready, 1)

        @block.vector
        def _(dve):
            steps = Steps(dve, vec)
            dve.wait_ge(x_in, 16)
            for t in range(TOKEN_TILES):
                last = dve.bn_stats(nx.stats[:, t, :], X[:, t, :])
            steps.link(last)
            norm_moments(dve, steps, nx, 0, TOKEN_TILES)
            norm_rstd(dve, steps, nx, 0, TOKEN_TILES, 1)
            for t in range(TOKEN_TILES):
                last = normalize(dve, lat[:, t, :], X[:, t, :], nx, t)
            steps.link(last)
            for t in range(TOKEN_TILES):
                last = dve.bn_stats(nl.stats[:, t, :], lat[:, t, :])
            steps.link(last)
            norm_moments(dve, steps, nl, 0, TOKEN_TILES)
            norm_rstd(dve, steps, nl, 0, TOKEN_TILES, 1)
            for n in range(CL):
                dve.wait_ge(ctx_in[n], 16)
                for t in range(n * PER, (n + 1) * PER):
                    last = dve.bn_stats(nk.stats[:, t, :], ctx[:, t, :])
                steps.link(last)
                norm_moments(dve, steps, nk, n * PER, (n + 1) * PER)
            dve.wait_ge(tail_in, 16)
            steps.link(dve.bn_stats(nk.stats[0:TAIL, CTX_TILES, :], tail[:, :]))
            norm_moments(dve, steps, nk, CTX_TILES, CTX_TILES + 1, TAIL)
            norm_rstd(dve, steps, nk, 0, CTX_TILES, CL)
            norm_rstd(dve, steps, nk, CTX_TILES, CTX_TILES + 1, CL + 1, TAIL)

            def low_parts(c):
                dve.wait_ge(full_ready, c + 1)
                dve.wait_ge(high_ready, c + 1)
                k = slice(c * BANK, c * BANK + width(c))
                dve.tensor_tensor(kvl[:, k], full[:, c % NF, 0:width(c)], kvh[:, k], op=ALU.subtract)\
                   .then_inc(low_ready, 1)

            for c in range(K_CHUNKS):
                for t in tiles_of(c):
                    if t < CTX_TILES:
                        i = normalize(dve, ctx[:, t, :], ctx[:, t, :], nk, t)
                    elif t < FULL_TILES:
                        i = normalize(dve, lat[:, t - CTX_TILES, :], lat[:, t - CTX_TILES, :], nl, t - CTX_TILES)
                    else:
                        i = normalize(dve, tail[:, :], tail[:, :], nk, CTX_TILES, TAIL)
                    i.then_inc(tile_ready, 1)
                if c >= 2:
                    low_parts(c - 2)
            low_parts(K_CHUNKS - 2)
            low_parts(K_CHUNKS - 1)
            dve.wait_ge(w_high, 5)
            for r in range(2):
                dve.tensor_tensor(pers.wk_l[:, :, r, :], wkv[:, 0:1024].rearrange("p (h d) -> p h d", d=DH),
                                  pers.wk_h[:, :, r, :], op=ALU.subtract).then_inc(w_done, 1)
                dve.tensor_tensor(pers.wq_l[:, :, r, :], wq[:, :].rearrange("p (h d) -> p h d", d=DH),
                                  pers.wq_h[:, :, r, :], op=ALU.subtract).then_inc(w_done, 1)
            dve.tensor_tensor(pers.wv_l[:, :], wkv[:, 1024:2048], pers.wv_h[:, :], op=ALU.subtract)\
               .then_inc(w_done, 1)

        @block.tensor
        def _(pe):
            pe.wait_ge(ident_ready, 1)
            for c in range(K_CHUNKS):
                if c >= NF:
                    pe.wait_ge(high_ready, c - NF + 1)
                for t in tiles_of(c):
                    pe.wait_ge(tile_ready, t + 1)
                    n = TAIL if t == FULL_TILES else P
                    src = ctx[:, t, :] if t < CTX_TILES else lat[:, t - CTX_TILES, :] if t < FULL_TILES else tail[:, :]
                    last = pe.transpose(T[c % NF][:, (t % 4) * P:(t % 4) * P + n], src, ident[0:n, 0:n])
                last.then_inc(transposed, 1)


def stage_attention(nc, pers, A):
    sc = Scope(nc, "att", pers.whole)
    with sc:
        kc = sc.sb("kc", [P, 2, KEY_COLS], F16)
        kd = sc.sb("kd", [P, 2, KEY_COLS], F16)
        v = sc.sb("v", [P, 2, KEY_TILES, VCOLS], F16)
        qc = sc.sb("qc", [P, 2, TOKENS], F16)
        qd = sc.sb("qd", [P, 2, TOKENS], F16)
        prob = [sc.sb(f"prob{n}", [P, TOKENS]) for n in range(2)]
        prob_low = [sc.sb(f"prob_low{n}", [P, TOKENS], F16) for n in range(2)]
        scores16 = [sc.sb(f"scores16_{n}", [P, 2 * BANK], BF16) for n in range(2)]
        running = [sc.sb(f"running{n}", [P, 2 * BANK], BF16) for n in range(2)]
        loop_max = sc.sb("loop_max", [P, TOKEN_TILES])
        rest_max = sc.sb("rest_max", [P, TOKEN_TILES])
        top = sc.sb("top", [P, TOKEN_TILES])
        rden = sc.sb("rden", [P, TOKEN_TILES])
        zeros = sc.sb("zeros", [P, BANK], F16)
        warm = sc.sb("warm", [1, 1])
        S = [pers.banks[:, 2 * n:2 * n + 2, :].rearrange("p b q -> p (b q)") for n in range(2)]
        X = pers.banks[:, 4:6, :]
        O = pers.banks[:, 6:8, :]
        SLOT_BANKS = [X, pers.banks[:, 0:2, :]]
        names = ("k_projected k_high k_split v_projected v_high v_split q_projected q_high q_split constants "
                 "scored exp_done prob_split applied max_scored max_copied max_taken folded max_reduced rest_scored "
                 "rest_reduced top_ready top_spread top_placed inverted normalized").split()
        s = {n: sc.sem(n) for n in names}
        (k_projected, k_high, k_split, v_projected, v_high, v_split, q_projected, q_high, q_split, constants,
         scored, exp_done, prob_split, applied, max_scored, max_copied, max_taken, folded, max_reduced, rest_scored,
         rest_reduced, top_ready, top_spread, top_placed, inverted, normalized) = (s[n] for n in names)
        kvh, kvl, ident, att = pers.kvh, pers.kvl, pers.ident, pers.att
        EXP0, NORM0, TAKEN0, REDUCED0 = 1, 1, 2, 2

        def dyn(i, size=1):
            return bass.ds(i, size)

        def kwidth(c):
            return min(BANK, KEYS - c * BANK)

        def bank(c):
            return S[1 - c % 4 // 2][:, (c % 2) * BANK:(c % 2) * BANK + kwidth(c)]

        def group(g):
            return list(range(8 * g, min(8 * g + 8, KEY_TILES)))

        def projection_order(first):
            order = [] if first else [("rest", REST_STEPS - 1)]
            order += [("k", c) for c in range(3)] + ([] if first else [("top", 0)])
            order += [("k", 3), ("k", 4), ("k", 5), ("q", 0), ("q", 1), ("k", 6), ("k", 7)]
            for c in range(8, K_CHUNKS):
                order += [("k", c), ("v", c - 8)]
            return order + ([("v", V_GROUPS - 1)] if first else [])

        block = sc.enter_context(nc.Block())

        @block.tensor
        def _(pe):
            def project_k(a, c, first):
                if c >= 4:
                    pe.wait_ge(k_split, a * K_CHUNKS + c - 3)
                elif not first:
                    pe.wait_ge(k_split, a * K_CHUNKS)
                    pe.wait_ge(exp_done, EXP0 + (a - 1) * KEY_TILES - (1 if c < 2 else 0))
                    pe.wait_ge(max_copied, a * MAX_SLOTS)
                r = kvh[:, c * BANK:c * BANK + kwidth(c)]
                rl = kvl[:, c * BANK:c * BANK + kwidth(c)]
                wh = pers.wk_h[:, dyn(a), :, :].rearrange("p a r d -> p (a r d)")
                wl = pers.wk_l[:, dyn(a), :, :].rearrange("p a r d -> p (a r d)")
                pe.matmul(bank(c), wh, r, start=True, stop=False)
                pe.matmul(bank(c), wh, rl, start=False, stop=False)
                pe.matmul(bank(c), wl, r, start=False, stop=True).then_inc(k_projected, 1)

            def project_v(a, g):
                if g >= 2:
                    pe.wait_ge(v_split, a * V_GROUPS + g - 1)
                else:
                    pe.wait_ge(q_split, a * 4 + 2 * g + 2)
                wh = pers.wv_h[:, dyn(a * DH, DH)]
                wl = pers.wv_l[:, dyn(a * DH, DH)]
                for t in group(g):
                    n = TAIL if t == FULL_TILES else P
                    o = X[0:n, g % 2, (t % 8) * DH:(t % 8 + 1) * DH]
                    th, tl = kvh[:, t * P:t * P + n], kvl[:, t * P:t * P + n]
                    pe.matmul(o, th, wh, start=True, stop=False)
                    pe.matmul(o, th, wl, start=False, stop=False)
                    last = pe.matmul(o, tl, wh, start=False, stop=True)
                last.then_inc(v_projected, 1)

            def project_q(a, i, first):
                if not first:
                    pe.wait_ge(top_placed, a)
                r = kvh[:, LATENT_COL + i * BANK:LATENT_COL + (i + 1) * BANK]
                rl = kvl[:, LATENT_COL + i * BANK:LATENT_COL + (i + 1) * BANK]
                wh = pers.wq_h[:, dyn(a), :, :].rearrange("p a r d -> p (a r d)")
                wl = pers.wq_l[:, dyn(a), :, :].rearrange("p a r d -> p (a r d)")
                pe.matmul(X[:, i, :], wh, r, start=True, stop=False)
                pe.matmul(X[:, i, :], wh, rl, start=False, stop=False)
                pe.matmul(X[:, i, :], wl, r, start=False, stop=True).then_inc(q_projected, 1)

            def project(a, first=False):
                for what, n in projection_order(first):
                    if what == "k":
                        project_k(a, n, first)
                    elif what == "rest":
                        rest_step(a - 1, n)
                    elif what == "top":
                        spread_top(a - 1)
                    elif what == "q":
                        project_q(a, n, first)
                    else:
                        project_v(a, n)

            def max_slot(m, j, c, slot, ready, banks=X, lead=0):
                if ready:
                    pe.wait_ge(k_split, (m + 1) * K_CHUNKS)
                    pe.wait_ge(q_split, (m + 1) * 4)
                    pe.wait_ge(v_split, (m + 1) * V_GROUPS)
                else:
                    pe.wait_ge(max_copied, m * MAX_SLOTS + slot - lead)
                par = m % 2
                lhs = qc[:, dyn(par), dyn(j * P, P)].rearrange("p a q -> p (a q)")
                for i in range(2):
                    rhs = kc[:, dyn(par), (2 * c + i) * BANK:(2 * c + i + 1) * BANK].rearrange("p a q -> p (a q)")
                    last = pe.matmul(banks[:, i, :], lhs, rhs, start=True, stop=True)
                last.then_inc(max_scored, 1)

            def rest_step(m, r):
                if r == 0:
                    pe.wait_ge(max_copied, (m + 1) * MAX_SLOTS)
                else:
                    pe.wait_ge(rest_reduced, m * REST_STEPS + r)
                par = m % 2
                for i in range(2):
                    j = 2 * r + i
                    lhs = qc[:, dyn(par), j * P:(j + 1) * P].rearrange("p a q -> p (a q)")
                    rhs = kc[:, dyn(par), REST_COL:KEYS].rearrange("p a q -> p (a q)")
                    last = pe.matmul(X[:, i, 0:REST], lhs, rhs, start=True, stop=True)
                last.then_inc(rest_scored, 1)

            def spread_top(m):
                pe.wait_ge(top_ready, m + 1)
                for j in range(TOKEN_TILES):
                    o = X[DH:P, j // 4, (j % 4) * P:(j % 4 + 1) * P]
                    last = pe.matmul(o, top[:, j:j + 1].to_broadcast([P, DH]), ident[:, :], start=True, stop=True)
                last.then_inc(top_spread, 1)

            def score(b, t, tile, after_projection):
                if after_projection is None:
                    pe.wait_ge(exp_done, EXP0 + b * KEY_TILES + tile - 1)
                elif after_projection:
                    pe.wait_ge(k_split, (b + 2) * K_CHUNKS)
                else:
                    pe.wait_ge(exp_done, EXP0 + b * KEY_TILES)
                par = b % 2
                st = S[t % 2]
                for lhs, rhs, start in ((kc, qc, True), (kd, qd, False)):
                    w = lhs[:, dyn(par), dyn(tile * P, P)].rearrange("p a q -> p (a q)")
                    for i in range(2):
                        r = rhs[:, dyn(par), i * BANK:(i + 1) * BANK].rearrange("p a q -> p (a q)")
                        last = pe.matmul(st[:, i * BANK:(i + 1) * BANK], w, r, start=start, stop=not start)
                last.then_inc(scored, 1)

            def wait_on_zeros():
                pe.matmul(O[:, 0, 0:DH], zeros[:, 0:P], zeros[:, 0:DH], start=False, stop=False, skip_group_check=True)

            def apply_high(b, t, tile, n=P):
                par = b % 2
                high = v[0:n, dyn(par), dyn(tile), 0:DH + 1].rearrange("p a t c -> p (a t c)")
                low = v[0:n, dyn(par), dyn(tile), DH + 1:VCOLS].rearrange("p a t c -> p (a t c)")
                pe.wait_ge(exp_done, EXP0 + b * KEY_TILES + tile + 1)
                if n < P:
                    wait_on_zeros()
                for j in range(TOKEN_TILES):
                    w = prob[t % 2][0:n, :].bitcast(BF16)[:, 2 * j * P + 1:2 * (j + 1) * P:2]
                    o = (j % 4) * (DH + 1)
                    pe.matmul(O[:, j // 4, o:o + DH + 1], w, high, start=False, stop=False, skip_group_check=True)
                    pe.matmul(O[:, j // 4, o:o + DH], w, low, start=False, stop=False, skip_group_check=True)

            def apply_low(b, t, tile, n=P):
                high = v[0:n, dyn(b % 2), dyn(tile), 0:DH + 1].rearrange("p a t c -> p (a t c)")
                pe.wait_ge(prob_split, b * KEY_TILES + tile + 1)
                if n < P:
                    wait_on_zeros()
                for j in range(TOKEN_TILES):
                    w = prob_low[t % 2][0:n, j * P:(j + 1) * P]
                    o = (j % 4) * (DH + 1)
                    last = pe.matmul(O[:, j // 4, o:o + DH + 1], w, high, start=False, stop=True,
                                     skip_group_check=True)
                last.then_inc(applied, 1)

            def attend(b, with_max):
                m = b + 1
                pe.wait_ge(top_placed, b + 1)
                pe.wait_ge(normalized, NORM0 + b)
                for i in range(2):
                    pe.matmul(O[:, i, :], zeros[:, 0:P], zeros[:, :], start=True, stop=False, skip_group_check=True)
                score(b, 0, 0, with_max)
                if with_max:
                    project_v(m, V_GROUPS - 1)
                score(b, 1, 1, with_max)
                pe.wait_ge(v_split, (b + 1) * V_GROUPS)

                def tile_step(t, tile, slot, ready):
                    apply_high(b, t, tile)
                    if with_max:
                        max_slot(m, slot[0], slot[1], slot[2], ready)
                    apply_low(b, t, tile)
                    score(b, t, tile + 2, None)

                for u in range(BODY):
                    tile_step(u, u, (u // MAX_CHUNKS, u % MAX_CHUNKS, u), u == 0)
                with pe.Fori(1, BODIES) as jj:
                    for u in range(BODY):
                        tile_step(u, jj * BODY + u, (jj * 2 + u // MAX_CHUNKS, u % MAX_CHUNKS, jj * BODY + u), False)
                for t in range(LOOP_TILES, KEY_TILES):
                    n = TAIL if t == FULL_TILES else P
                    apply_high(b, t, t, n)
                    if with_max:
                        rest_step(m, t - LOOP_TILES)
                    apply_low(b, t, t, n)
                    if t + 2 < KEY_TILES:
                        score(b, t, t + 2, None)

            pe.wait_ge(constants, 5)
            project(0, first=True)
            for u in range(BODY):
                max_slot(0, u // MAX_CHUNKS, u % MAX_CHUNKS, u, u < 2, SLOT_BANKS[u % 2], 1)
            with pe.Fori(1, BODIES) as jj:
                for u in range(BODY):
                    max_slot(0, jj * 2 + u // MAX_CHUNKS, u % MAX_CHUNKS, jj * BODY + u, False, SLOT_BANKS[u % 2], 1)
            for r in range(REST_STEPS - 1):
                rest_step(0, r)
            with pe.Fori(0, HEADS - 1) as h:
                project(h + 1)
                attend(h, True)
            rest_step(HEADS - 1, REST_STEPS - 1)
            spread_top(HEADS - 1)
            attend(HEADS - 1, False)

        @block.scalar
        def _(act):
            def project(a, first=False):
                par = a % 2
                for what, n in projection_order(first):
                    if what == "k":
                        act.wait_ge(k_projected, a * K_CHUNKS + n + 1)
                        o = kc[:, dyn(par), n * BANK:n * BANK + kwidth(n)].rearrange("p a q -> p (a q)")
                        act.activation(o, bank(n), ACT.Copy).then_inc(k_high, 1)
                    elif what == "q":
                        act.wait_ge(q_projected, a * 2 + n + 1)
                        o = qc[:, dyn(par), n * BANK:(n + 1) * BANK].rearrange("p a q -> p (a q)")
                        act.activation(o, X[:, n, :], ACT.Copy).then_inc(q_high, 1)
                    elif what == "v":
                        copy_v(a, n)
                    elif what == "top":
                        place_top(a - 1)

            def copy_v(a, n):
                par = a % 2
                act.wait_ge(v_projected, a * V_GROUPS + n + 1)
                whole = [t for t in group(n) if t < FULL_TILES]
                w = len(whole)
                o = v[:, dyn(par), whole[0]:whole[0] + w, 0:DH].rearrange("p a t c -> p (a t) c")
                last = act.activation(o, X[:, n % 2, 0:w * DH].rearrange("p (t c) -> p t c", c=DH), ACT.Copy)
                if w < len(group(n)):
                    o = v[0:TAIL, dyn(par), FULL_TILES, 0:DH].rearrange("p a c -> p (a c)")
                    last = act.activation(o, X[0:TAIL, n % 2, w * DH:(w + 1) * DH], ACT.Copy)
                last.then_inc(v_high, 1)

            def place_top(m):
                act.wait_ge(top_spread, m + 1)
                o = qd[DH:P, dyn(m % 2), :].rearrange("p a q -> p (a q)")
                act.activation(o, X[DH:P, :, :].rearrange("p a q -> p (a q)"), ACT.Copy, scale=-1.0, bias=LIFT)\
                   .then_inc(top_placed, 1)

            def copy_slot(m, j, half, c, slot, banks=X):
                act.wait_ge(max_scored, m * MAX_SLOTS + slot + 1)
                if c == 0:
                    act.wait_ge(max_reduced, m * TOKEN_TILES + j - 1 + REDUCED0)
                    o = running[half]
                else:
                    act.wait_ge(max_taken, (m * TOKEN_TILES + j) * (MAX_CHUNKS - 1) + c - 2 + TAKEN0)
                    o = scores16[c % 2]
                act.activation(o[:, :], banks[:, :, :].rearrange("p a q -> p (a q)"), ACT.Copy).then_inc(max_copied, 1)

            def exp(b, t, tile, n=P):
                act.wait_ge(scored, b * KEY_TILES + tile + 1)
                if t >= 2:
                    act.wait_ge(applied, b * KEY_TILES + tile - 1)
                act.activation(prob[t % 2][0:n, :], S[t % 2][0:n, :], ACT.Exp, scale=SCALE).then_inc(exp_done, 1)

            def attend(b, with_max):
                m = b + 1
                if with_max:
                    copy_v(m, V_GROUPS - 1)
                exp(b, 0, 0)
                for u in range(BODY):
                    exp(b, u + 1, u + 1)
                    if with_max:
                        copy_slot(m, u // MAX_CHUNKS, u // MAX_CHUNKS, u % MAX_CHUNKS, u)
                with act.Fori(1, BODIES) as jj:
                    for u in range(BODY):
                        exp(b, BODY + u + 1, jj * BODY + u + 1)
                        if with_max:
                            copy_slot(m, jj * 2 + u // MAX_CHUNKS, u // MAX_CHUNKS, u % MAX_CHUNKS, jj * BODY + u)
                for t in range(LOOP_TILES + 1, KEY_TILES):
                    exp(b, t, t, TAIL if t == FULL_TILES else P)

            act.wait_ge(constants, 1)
            act.activation(warm[:, :], zeros[0:1, 0:1], ACT.Exp).then_inc(exp_done, 1)
            project(0, first=True)
            for u in range(BODY):
                copy_slot(0, u // MAX_CHUNKS, u // MAX_CHUNKS, u % MAX_CHUNKS, u, SLOT_BANKS[u % 2])
            with act.Fori(1, BODIES) as jj:
                for u in range(BODY):
                    copy_slot(0, jj * 2 + u // MAX_CHUNKS, u // MAX_CHUNKS, u % MAX_CHUNKS, jj * BODY + u,
                              SLOT_BANKS[u % 2])
            with act.Fori(0, HEADS - 1) as h:
                project(h + 1)
                attend(h, True)
            place_top(HEADS - 1)
            attend(HEADS - 1, False)

        @block.vector
        def _(dve):
            def split_k(a, c):
                par = a % 2
                dve.wait_ge(k_high, a * K_CHUNKS + c + 1)
                k = slice(c * BANK, c * BANK + kwidth(c))
                o = kd[0:DH, dyn(par), k].rearrange("p a q -> p (a q)")
                h = kc[0:DH, dyn(par), k].rearrange("p a q -> p (a q)")
                dve.tensor_tensor(o, bank(c)[0:DH, :], h, op=ALU.subtract).then_inc(k_split, 1)

            def split_v(a, g):
                par = a % 2
                dve.wait_ge(v_high, a * V_GROUPS + g + 1)
                whole = [t for t in group(g) if t < FULL_TILES]
                n = len(whole)
                tt = slice(whole[0], whole[0] + n)
                o = v[:, dyn(par), tt, DH + 1:VCOLS].rearrange("p a t c -> p (a t) c")
                h = v[:, dyn(par), tt, 0:DH].rearrange("p a t c -> p (a t) c")
                x = X[:, g % 2, 0:n * DH].rearrange("p (t c) -> p t c", c=DH)
                last = dve.tensor_tensor(o, x, h, op=ALU.subtract)
                if n < len(group(g)):
                    o = v[0:TAIL, dyn(par), FULL_TILES, DH + 1:VCOLS].rearrange("p a c -> p (a c)")
                    h = v[0:TAIL, dyn(par), FULL_TILES, 0:DH].rearrange("p a c -> p (a c)")
                    last = dve.tensor_tensor(o, X[0:TAIL, g % 2, n * DH:(n + 1) * DH], h, op=ALU.subtract)
                last.then_inc(v_split, 1)

            def split_q(a, i):
                par = a % 2
                dve.wait_ge(q_high, a * 2 + i + 1)
                k = slice(i * BANK, (i + 1) * BANK)
                top_half = qc[0:DH, dyn(par), k].rearrange("p a q -> p (a q)")
                low_half = qc[DH:P, dyn(par), k].rearrange("p a q -> p (a q)")
                dve.tensor_copy(qd[0:DH, dyn(par), k].rearrange("p a q -> p (a q)"), top_half).then_inc(q_split, 1)
                dve.tensor_tensor(low_half, X[DH:P, i, :], low_half, op=ALU.subtract).then_inc(q_split, 1)

            def project(a, first=False):
                for what, n in projection_order(first):
                    if what == "k":
                        split_k(a, n)
                    elif what == "rest":
                        rest_step(a - 1, n)
                        finish_max(a - 1)
                    elif what == "q":
                        split_q(a, n)
                    elif what == "v":
                        split_v(a, n)

            def take_slot(m, j, half, c, slot, fold=True):
                dve.wait_ge(max_copied, m * MAX_SLOTS + slot + 1)
                r = running[half]
                if c:
                    taken = (m * TOKEN_TILES + j) * (MAX_CHUNKS - 1) + c + TAKEN0
                    if c > 1:
                        dve.wait_ge(max_taken, taken - 1)
                    dve.tensor_tensor(r[:, :], r[:, :], scores16[c % 2][:, :], op=ALU.max).then_inc(max_taken, 1)
                if c == MAX_CHUNKS - 1 and fold:
                    fold_tile(m, j, half)

            def fold_tile(m, j, half):
                r = running[half]
                dve.wait_ge(max_taken, (m * TOKEN_TILES + j + 1) * (MAX_CHUNKS - 1) + TAKEN0)
                dve.tensor_tensor(r[:, 0:BANK], r[:, 0:BANK], r[:, BANK:2 * BANK], op=ALU.max).then_inc(folded, 1)
                dve.wait_ge(folded, m * TOKEN_TILES + j + 1)
                dve.tensor_reduce(loop_max[:, dyn(j)], r[:, 0:BANK], axis=AX.X, op=ALU.max).then_inc(max_reduced, 1)

            def rest_step(m, r):
                dve.wait_ge(rest_scored, m * REST_STEPS + r + 1)
                dve.tensor_reduce(rest_max[:, 2 * r:2 * r + 2], X[:, :, 0:REST], axis=AX.X, op=ALU.max)\
                   .then_inc(rest_reduced, 1)

            def finish_max(m):
                dve.wait_ge(rest_reduced, (m + 1) * REST_STEPS)
                dve.wait_ge(max_reduced, (m + 1) * TOKEN_TILES + REDUCED0)
                dve.tensor_tensor(top[:, :], loop_max[:, :], rest_max[:, :], op=ALU.max).then_inc(top_ready, 1)

            def split(b, t, tile, n=P):
                dve.wait_ge(exp_done, EXP0 + b * KEY_TILES + tile + 1)
                p = prob[t % 2][0:n, :]
                dve.tensor_tensor(prob_low[t % 2][0:n, :], p, p.bitcast(BF16)[:, 1:2 * TOKENS:2], op=ALU.subtract)\
                   .then_inc(prob_split, 1)

            def take_before(m, jj, u, fold=True):
                if u:
                    take_slot(m, jj * 2 + (u - 1) // MAX_CHUNKS, (u - 1) // MAX_CHUNKS, (u - 1) % MAX_CHUNKS,
                              jj * BODY + u - 1)
                else:
                    take_slot(m, jj * 2 - 1, 1, MAX_CHUNKS - 1, jj * BODY - 1, fold)

            def attend(b, with_max):
                m = b + 1
                if with_max:
                    split_v(m, V_GROUPS - 1)
                for u in range(BODY):
                    split(b, u, u)
                    if with_max and u:
                        take_before(m, 0, u)
                with dve.Fori(1, BODIES) as jj:
                    for u in range(BODY):
                        split(b, u, jj * BODY + u)
                        if with_max:
                            take_before(m, jj, u)
                for t in range(LOOP_TILES, KEY_TILES):
                    split(b, t, t, TAIL if t == FULL_TILES else P)
                    if with_max:
                        if t == LOOP_TILES:
                            take_before(m, BODIES, 0, fold=False)
                        rest_step(m, t - LOOP_TILES)
                if with_max:
                    fold_tile(m, TOKEN_TILES - 1, 1)
                dve.wait_ge(applied, (b + 1) * KEY_TILES)
                sums = O[:, :, 0:4 * (DH + 1)].rearrange("p b (j c) -> p b j c", c=DH + 1)
                r = rden[:, :].rearrange("p (b j) -> p b j", b=2)
                dve.reciprocal(r, sums[:, :, :, DH]).then_inc(inverted, 1)
                dve.wait_ge(inverted, b + 1)
                for i in range(2):
                    o = att[:, 4 * i:4 * i + 4, dyn(b * DH, DH)]
                    last = dve.tensor_tensor(o, sums[:, i, :, 0:DH], spread_columns(rden[:, 4 * i:4 * i + 4], DH),
                                             op=ALU.mult)
                last.then_inc(normalized, 1)

            dve.memset(zeros[:, :], 0.0).then_inc(constants, 1)
            dve.memset(kd[DH:P, :, :], 1.0 / DH).then_inc(constants, 1)
            dve.memset(kd[0:DH, :, KEYS:KEY_COLS], 0.0).then_inc(constants, 1)
            dve.memset(kc[:, :, KEYS:KEY_COLS], 0.0).then_inc(constants, 1)
            dve.memset(v[:, :, :, DH:DH + 1], 1.0).then_inc(constants, 1)
            dve.memset(top[:, 0:1], 0.0).then_inc(normalized, NORM0)
            dve.memset(top[:, 1:2], 0.0).then_inc(max_taken, TAKEN0)
            dve.memset(top[:, 2:3], 0.0).then_inc(max_reduced, REDUCED0)
            dve.wait_ge(normalized, 1)
            dve.wait_ge(max_taken, TAKEN0)
            dve.wait_ge(max_reduced, REDUCED0)
            project(0, first=True)
            for u in range(BODY):
                take_slot(0, u // MAX_CHUNKS, u // MAX_CHUNKS, u % MAX_CHUNKS, u)
            with dve.Fori(1, BODIES) as jj:
                for u in range(BODY):
                    take_slot(0, jj * 2 + u // MAX_CHUNKS, u // MAX_CHUNKS, u % MAX_CHUNKS, jj * BODY + u)
            for r in range(REST_STEPS - 1):
                rest_step(0, r)
            with dve.Fori(0, HEADS - 1) as h:
                project(h + 1)
                attend(h, True)
            rest_step(HEADS - 1, REST_STEPS - 1)
            finish_max(HEADS - 1)
            attend(HEADS - 1, False)


def stage_attention_out(nc, pers, A):
    sc = Scope(nc, "wout", pers.whole)
    KT = HEADS * DH // P
    with sc:
        wout = sc.sb("w", [P, KT, D])
        att_t = [sc.sb(f"att_t{n}", [P, KT, P]) for n in range(2)]
        T = [pers.banks[:, 2 * n:2 * n + 2, :].rearrange("p b (k q) -> p (b k) q", q=P) for n in range(2)]
        Y = [pers.banks[:, 4 + n, 0:D] for n in range(2)]
        w_in, transposed, front_copied, back_copied, multiplied, added = (
            sc.sem(n) for n in ("w_in", "transposed", "front_copied", "back_copied", "multiplied", "added"))
        X, att, ident = pers.X, pers.att, pers.ident
        block = sc.enter_context(nc.Block())

        @block.sync
        def _(sp):
            sp.dma_start(wout[:, :, :], A["wout"].rearrange("(k p) d -> p k d", p=P)).then_inc(w_in, 16)

        @block.tensor
        def _(pe):
            def transpose(j):
                if j >= 2:
                    pe.wait_ge(front_copied, j - 1)
                    pe.wait_ge(back_copied, j - 1)
                for k in range(KT):
                    last = pe.transpose(T[j % 2][:, k, :], att[:, j, k * P:(k + 1) * P], ident[:, :])
                last.then_inc(transposed, 1)

            transpose(0)
            pe.wait_ge(w_in, 16)
            for j in range(TOKEN_TILES):
                if j + 1 < TOKEN_TILES:
                    transpose(j + 1)
                pe.wait_ge(front_copied, j + 1)
                pe.wait_ge(back_copied, j + 1)
                if j >= 2:
                    pe.wait_ge(added, j - 1)
                for k in range(KT):
                    last = pe.matmul(Y[j % 2][:, :], att_t[j % 2][:, k, :], wout[:, k, :], start=k == 0,
                                     stop=k == KT - 1)
                last.then_inc(multiplied, 1)

        def copy(eng, j, half):
            eng.wait_ge(transposed, j + 1)
            if j >= 2:
                eng.wait_ge(multiplied, j - 1)
            k = slice(half * KT // 2, (half + 1) * KT // 2)
            return att_t[j % 2][:, k, :], T[j % 2][:, k, :]

        @block.scalar
        def _(act):
            for j in range(TOKEN_TILES):
                o, i = copy(act, j, 0)
                act.activation(o, i, ACT.Copy).then_inc(front_copied, 1)

        @block.vector
        def _(dve):
            for j in range(TOKEN_TILES + 1):
                if j < TOKEN_TILES:
                    o, i = copy(dve, j, 1)
                    dve.tensor_copy(o, i).then_inc(back_copied, 1)
                if j >= 1:
                    dve.wait_ge(multiplied, j)
                    dve.tensor_tensor(X[:, j - 1, :], Y[(j - 1) % 2][:, :], X[:, j - 1, :], op=ALU.add)\
                       .then_inc(added, 1)


def stage_experts(nc, pers, A, name, layer, out=None):
    sc = Scope(nc, name, pers.whole)
    second = layer == 1
    W = P // GROUP
    with sc:
        n = sc.sb("n", [P, TOKEN_TILES, D])
        n_t = sc.sb("n_t", [P, TOKENS])
        control = sc.sb("control", [P, ES])
        up = sc.sb("up", [P, ES, ESIZE])
        down = sc.sb("down", [P, EXPERTS, D])
        up_bias = sc.sb("up_bias", [EXPERTS, P])
        up_bias_t = sc.sb("up_bias_t", [P, EXPERTS])
        tie = sc.sb("tie", [P, GROUP])
        logits = sc.sb("logits", [P, GROUPS, GROUP])
        largest = sc.sb("largest", [P, GROUPS])
        pick_t = sc.sb("pick_t", [P, GROUPS, GROUP])
        pick = sc.sb("pick", [P, TOKEN_TILES, ES])
        taken_t = sc.sb("taken_t", [P, GROUPS, ES])
        hidden = sc.sb("hidden", [P, EXPERTS, SETS, GROUPS])
        biased = sc.sb("biased", [P, EXPERTS, GROUPS])
        result_t = sc.sb("result_t", [P, ES, GROUPS])
        result = sc.sb("result", [P, GROUPS, D])
        if second:
            control_bias = sc.sb("control_bias", [P, 1])
            down_bias = sc.sb("down_bias", [P, D])
            down_raw = sc.sb("down_raw", [P, EXPERTS, SETS * ESIZE])
        ns = NormState(sc, "ns", TOKEN_TILES)
        NB = 8
        B = [pers.banks[:, i, :] for i in range(NB)]
        names = ("control_in up_in down_in bias_in tie_ready vec normalized transposed copied scored picked "
                 "pick_transposed pick_copied took took_copied up_done hidden_zeroed biased_ready hidden_front hidden_back bias_transposed "
                 "bias_copied down_transposed down_copied down_done down_read result_transposed result_copied "
                 "returned added stored").split()
        s = {x: sc.sem(x) for x in names}
        X, ident = pers.X, pers.ident
        block = sc.enter_context(nc.Block())

        @block.sync
        def _(sp):
            sp.dma_start(control[:, :], A["control"].rearrange("d e s -> d (e s)")).then_inc(s["control_in"], 16)
            if second:
                sp.dma_start(control_bias[:, :], A["control_bias"].rearrange("e (s one) -> (e s) one", one=1))\
                  .then_inc(s["control_in"], 16)
                sp.dma_start(up[:, :, :], A["up"].rearrange("e s d f -> d (e s) f")).then_inc(s["up_in"], 16)
            else:
                sp.dma_start(up[:, :, :], A["up"].rearrange("d e s f -> d (e s) f")).then_inc(s["up_in"], 16)
            if out is not None:
                view = out[0].rearrange("(t p) d -> p t d", p=P)
                for i in range(2):
                    sp.wait_ge(s["added"], i + 1)
                    sp.dma_start(view[:, 4 * i:4 * i + 4, :], X[:, 4 * i:4 * i + 4, :]).then_inc(s["stored"], 16)
                sp.wait_ge(s["stored"], 32)

        @block.gpsimd
        def _(pool):
            for t in range(GROUP):
                last = pool.memset(tie[:, t:t + 1], t * TIE_STEP)
            last.then_inc(s["tie_ready"], 1)
            pool.memset(hidden[:, :, :, :], 0.0).then_inc(s["hidden_zeroed"], 1)

        @block.scalar
        def _(act):
            act.dma_start(up_bias[:, :], A["up_bias"].rearrange("e s f -> e (s f)")).then_inc(s["bias_in"], 16)
            if second:
                act.dma_start(down_raw[:, :, :].rearrange("p e (s f) -> p (e s) f", f=ESIZE),
                              A["down"].rearrange("e s d f -> d (e s) f")).then_inc(s["down_in"], 16)
                act.dma_start(down_bias[:, :], A["down_bias"].rearrange("e s d -> (e s) d")).then_inc(s["bias_in"], 16)
            else:
                act.dma_start(down[:, :, :], A["down"].rearrange("e s f d -> (s f) e d")).then_inc(s["down_in"], 16)
            norm_sqrt(act, ns, 0, TOKEN_TILES, 1)
            for i in range(2):
                act.wait_ge(s["transposed"], i + 1)
                act.activation(n_t[:, i * BANK:(i + 1) * BANK], B[i][:, :], ACT.Copy).then_inc(s["copied"], 1)
            act.wait_ge(s["bias_transposed"], 1)
            act.activation(up_bias_t[:, :], B[6][:, 0:EXPERTS], ACT.Copy).then_inc(s["bias_copied"], 1)
            if second:
                for k in range(EXPERTS // W):
                    act.wait_ge(s["down_transposed"], k + 1)
                    act.activation(down[:, 4 * k:4 * k + 4, :], B[6 + k % 2][:, :].rearrange("p (e d) -> p e d", d=D),
                                   ACT.Copy).then_inc(s["down_copied"], 1)
            for i in range(2):
                act.wait_ge(s["pick_transposed"], i + 1)
                act.activation(pick[:, 4 * i:4 * i + 4, :], B[i][:, :].rearrange("p (t c) -> p t c", c=ES), ACT.Copy)\
                   .then_inc(s["pick_copied"], 1)
            act.wait_ge(s["biased_ready"], 2)
            act.wait_ge(s["hidden_zeroed"], 1)
            for q in (0, 1):
                r = slice(q * ESIZE, (q + 1) * ESIZE)
                last = act.activation(hidden[r, :, q, :], biased[r, :, :], ACT.Relu)
            last.then_inc(s["hidden_front"], 1)
            for k in range(EXPERTS // W):
                act.wait_ge(s["down_done"], k + 1)
                act.activation(result_t[:, k * 4 * SETS:(k + 1) * 4 * SETS, :],
                               B[k % 4][:, :].rearrange("p (c g) -> p c g", g=GROUPS), ACT.Copy)\
                   .then_inc(s["down_read"], 1)

        @block.vector
        def _(dve):
            steps = Steps(dve, s["vec"])
            for t in range(TOKEN_TILES):
                last = dve.bn_stats(ns.stats[:, t, :], X[:, t, :])
            steps.link(last)
            norm_moments(dve, steps, ns, 0, TOKEN_TILES)
            norm_rstd(dve, steps, ns, 0, TOKEN_TILES, 1)
            for t in range(TOKEN_TILES):
                normalize(dve, n[:, t, :], X[:, t, :], ns, t).then_inc(s["normalized"], 1)
            dve.wait_ge(s["tie_ready"], 1)
            if second:
                dve.wait_ge(s["control_in"], 32)
            H = GROUPS // 2
            tied = tie[:, :].rearrange("p (one t) -> p one t", one=1).to_broadcast([P, H, GROUP])
            for i in range(2):
                dve.wait_ge(s["scored"], i + 1)
                g = slice(i * H, (i + 1) * H)
                bias = control_bias[:, 0:1] if second else 0.0
                steps.link(dve.scalar_tensor_tensor(logits[:, g, :], B[2 + i][:, :].rearrange("p (g t) -> p g t", t=GROUP),
                                                    bias, tied, ALU.add, ALU.add))
                steps.link(dve.tensor_reduce(largest[:, g], logits[:, g, :], axis=AX.X, op=ALU.max))
                dve.tensor_tensor(pick_t[:, g, :], logits[:, g, :], spread_columns(largest[:, g], GROUP),
                                  op=ALU.is_equal).then_inc(s["picked"], 1)
            by_tile = taken_t[:, :, :].rearrange("p (j g) c -> p g j c", g=W)
            for x in range(2 * W):
                half, g = x // W, x % W
                dve.wait_ge(s["took"], x + 1)
                dve.tensor_copy(by_tile[:, g, 4 * half:4 * half + 4, :],
                                B[2 + g][:, :].rearrange("p (j c) -> p j c", c=ES)).then_inc(s["took_copied"], 1)
            dve.wait_ge(s["bias_copied"], 1)
            for i in range(2):
                dve.wait_ge(s["up_done"], i + 1)
                e = slice(i * EXPERTS // 2, (i + 1) * EXPERTS // 2)
                dve.tensor_tensor(biased[:, e, :], B[i][:, :].rearrange("p (e g) -> p e g", g=GROUPS),
                                  spread_columns(up_bias_t[:, e], GROUPS), op=ALU.add).then_inc(s["biased_ready"], 1)
            dve.wait_ge(s["biased_ready"], 2)
            dve.wait_ge(s["hidden_zeroed"], 1)
            for q in (2, 3):
                r = slice(q * ESIZE, (q + 1) * ESIZE)
                last = dve.tensor_scalar(hidden[r, :, q, :], biased[r, :, :], 0.0, None, ALU.max)
            last.then_inc(s["hidden_back"], 1)
            for k in range(GROUPS // 4):
                dve.wait_ge(s["result_transposed"], k + 1)
                o = result[:, 4 * k:4 * k + 4, :]
                i_ = B[4 + k % 2][:, :].rearrange("p (g d) -> p g d", d=D)
                if second:
                    if k == 0:
                        dve.wait_ge(s["bias_in"], 32)
                    b = down_bias[:, :].rearrange("p (one d) -> p one d", one=1).to_broadcast([P, 4, D])
                    dve.tensor_tensor(o, i_, b, op=ALU.add).then_inc(s["result_copied"], 1)
                else:
                    dve.tensor_copy(o, i_).then_inc(s["result_copied"], 1)
            for i in range(2):
                dve.wait_ge(s["returned"], i + 1)
                x = X[:, 4 * i:4 * i + 4, :]
                dve.tensor_tensor(x, B[6 + i][:, :].rearrange("p (t d) -> p t d", d=D), x, op=ALU.add)\
                   .then_inc(s["added"], 1)

        @block.tensor
        def _(pe):
            for t in range(TOKEN_TILES):
                pe.wait_ge(s["normalized"], t + 1)
                last = pe.transpose(B[t // 4][:, (t % 4) * P:(t % 4 + 1) * P], n[:, t, :], ident[:, :])
                if t % 4 == 3:
                    last.then_inc(s["transposed"], 1)
            pe.wait_ge(s["control_in"], 32 if second else 16)
            for i in range(2):
                pe.wait_ge(s["copied"], i + 1)
                pe.matmul(B[2 + i][:, :], control[:, :], n_t[:, i * BANK:(i + 1) * BANK], start=True, stop=True)\
                  .then_inc(s["scored"], 1)
            pe.wait_ge(s["bias_in"], 32 if second else 16)
            pe.transpose(B[6][:, 0:EXPERTS], up_bias[:, :], ident[0:EXPERTS, 0:EXPERTS]).then_inc(s["bias_transposed"], 1)
            if second:
                pe.wait_ge(s["down_in"], 16)
                for k in range(EXPERTS // W):
                    pe.wait_ge(s["bias_copied"], 1)
                    if k >= 2:
                        pe.wait_ge(s["down_copied"], k - 1)
                    for e in range(4):
                        last = pe.transpose(B[6 + k % 2][:, e * P:(e + 1) * P], down_raw[:, 4 * k + e, :], ident[:, :])
                    last.then_inc(s["down_transposed"], 1)
            for i in range(2):
                pe.wait_ge(s["picked"], i + 1)
                for t in range(4 * i, 4 * i + 4):
                    last = pe.transpose(B[i][:, (t % 4) * P:(t % 4 + 1) * P],
                                        pick_t[:, :, :].rearrange("p g t -> p (g t)")[:, t * P:(t + 1) * P], ident[:, :])
                last.then_inc(s["pick_transposed"], 1)
            for half in range(2):
                pe.wait_ge(s["pick_copied"], half + 1)
                for g in range(W):
                    r = slice(g * GROUP, (g + 1) * GROUP)
                    if half:
                        pe.wait_ge(s["took_copied"], g + 1)
                    for t in range(4):
                        j = 4 * half + t
                        last = pe.matmul(B[2 + g][:, t * ES:(t + 1) * ES], n[r, j, :], pick[r, j, :], start=True,
                                         stop=True)
                    last.then_inc(s["took"], 1)
            pe.wait_ge(s["up_in"], 16)
            pe.wait_ge(s["took_copied"], 2 * W)
            for c in range(ES):
                e, q = c // SETS, c % SETS
                o = B[e // 16][q * ESIZE:(q + 1) * ESIZE, (e % 16) * GROUPS:(e % 16 + 1) * GROUPS]
                last = pe.matmul(o, up[:, c, :], taken_t[:, :, c], start=True, stop=True)
                if c % (ES // 2) == ES // 2 - 1:
                    last.then_inc(s["up_done"], 1)
            pe.wait_ge(s["hidden_front"], 1)
            pe.wait_ge(s["hidden_back"], 1)
            if second:
                pe.wait_ge(s["down_copied"], EXPERTS // W)
            else:
                pe.wait_ge(s["down_in"], 16)
            for k in range(EXPERTS // W):
                if k >= 4:
                    pe.wait_ge(s["down_read"], k - 3)
                for e in range(4):
                    last = pe.matmul(B[k % 4][:, e * P:(e + 1) * P], down[:, 4 * k + e, :],
                                     hidden[:, 4 * k + e, :, :].rearrange("p s g -> p (s g)"), start=True, stop=True)
                last.then_inc(s["down_done"], 1)
            pe.wait_ge(s["down_read"], EXPERTS // W)
            for k in range(GROUPS // 4 + 1):
                if k < GROUPS // 4:
                    if k >= 2:
                        pe.wait_ge(s["result_copied"], k - 1)
                    for i in range(4):
                        last = pe.transpose(B[4 + k % 2][:, i * P:(i + 1) * P], result_t[:, :, 4 * k + i], ident[:, :])
                    last.then_inc(s["result_transposed"], 1)
                if k >= 1:
                    j = k - 1
                    pe.wait_ge(s["result_copied"], k)
                    for i in range(W):
                        g = 4 * j + i
                        last = pe.matmul(B[6 + j // 4][i * GROUP:(i + 1) * GROUP, (j % 4) * D:(j % 4 + 1) * D],
                                         pick_t[:, g, :], result[:, g, :], start=True, stop=True)
                    if j % 4 == 3:
                        last.then_inc(s["returned"], 1)


def stage_cross(nc, pers, A):
    sc = Scope(nc, "cross", pers.whole)
    QT = CTX_TILES + 1
    QC = -(-CONTEXT // BANK)
    PIECES = -(-QC // 2)
    AHEAD = 3
    SCORED_BY = QC - 1 - AHEAD
    APPLY_LAG = 2
    with sc:
        ctx = sc.sb("ctx", [P, CTX_TILES, D])
        tail = sc.sb("tail", [TAIL, D])
        ctx_h = sc.sb("ctx_h", [P, QT, D], F16)
        ctx_l = sc.sb("ctx_l", [P, QT, D], F16)
        q_h = sc.sb("q_h", [P, CONTEXT], F16)
        q_l = sc.sb("q_l", [P, CONTEXT], F16)
        c = sc.sb("c", [P, TOKEN_TILES, D])
        c_t = sc.sb("c_t", [P, TOKENS])
        m_t = sc.sb("m_t", [P, TOKENS])
        m_h = sc.sb("m_h", [P, TOKENS], F16)
        m_l = sc.sb("m_l", [P, TOKENS], F16)
        w = sc.sb("w", [P, 3])
        bs = sc.sb("bs", [P, 4])
        scores = sc.sb("scores", [P, 2, CONTEXT])
        NPT = 3
        pt_h = sc.sb("pt_h", [P, NPT, BANK], F16)
        pt_l = sc.sb("pt_l", [P, NPT, BANK], F16)
        chunk_max = sc.sb("chunk_max", [P, QC])
        top = sc.sb("top", [P, TOKEN_TILES])
        neg_top = sc.sb("neg_top", [P, TOKEN_TILES])
        den_parts = sc.sb("den_parts", [P, TOKEN_TILES, PIECES])
        den = sc.sb("den", [P, TOKEN_TILES])
        rden = sc.sb("rden", [P, TOKEN_TILES])
        c2q = sc.sb("c2q", [P, TOKEN_TILES, D])
        c2q_t = sc.sb("c2q_t", [P, TOKENS])
        mixed_t = sc.sb("mixed_t", [P, TOKENS])
        back_t = sc.sb("back_t", [P, TOKENS])
        wl = sc.sb("wl", [P, 4, P])
        wl_t = sc.sb("wl_t", [P, 4, P])
        bl = sc.sb("bl", [P, D])
        level = sc.sb("level", [P, TOKEN_TILES])
        level_max = sc.sb("level_max", [P, 1])
        all_max = sc.sb("all_max", [P, 1])
        neg_all_max = sc.sb("neg_all_max", [P, 1])
        row_max = sc.sb("row_max", [1, P])
        one_max = sc.sb("one_max", [1, 1])
        b_att = sc.sb("b_att", [P, TOKEN_TILES])
        ones = sc.sb("ones", [P, P])
        q2c = sc.sb("q2c", [P, 1])
        rsum = sc.sb("rsum", [P, 1])
        ns = NormState(sc, "ns", TOKEN_TILES)
        B = [pers.banks[:, i, :] for i in range(8)]
        names = ("ctx_in tail_in w_in bl_in vec normalized transposed copied m_ready m_high m_split q_transposed "
                 "q_high q_split rows_high rows_split scored stored max_ready exponents probs_t probs_high probs_split "
                 "applied applied_read ready_ones wl_transposed wl_copied level_done level_ready row_ready "
                 "row_taken one_ready spread spread_read weights_ready summed summed_read c2q_ready c2q_transposed "
                 "c2q_copied factors projected added").split()
        s = {x: sc.sem(x) for x in names}
        X, ident = pers.X, pers.ident
        block = sc.enter_context(nc.Block())

        def width(k):
            return min(BANK, CONTEXT - k * BANK)

        def tiles_of(k):
            return list(range(4 * k, min(4 * k + 4, QT)))

        def rows(t):
            return TAIL if t == CTX_TILES else P

        def spans(k):
            whole = len([t for t in tiles_of(k) if t < CTX_TILES])
            out = [(0, whole * P, P)] if whole else []
            if CTX_TILES in tiles_of(k):
                out.append((whole * P, (whole + 1) * P, TAIL))
            return out

        def scored_in(k):
            if k < AHEAD:
                return [2 * k, 2 * k + 1]
            return [k + AHEAD] if k <= SCORED_BY else []

        @block.sync
        def _(sp):
            sp.dma_start(ctx[:, :, :], A["ctx"][0, 0:CTX_ROWS, :].rearrange("(p t) d -> p t d", p=P)).then_inc(s["ctx_in"], 16)
            sp.dma_start(tail[:, :], A["ctx"][0, CTX_ROWS:CONTEXT, :]).then_inc(s["tail_in"], 16)

        @block.gpsimd
        def _(pool):
            pool.memset(ones[:, :], 1.0).then_inc(s["ready_ones"], 1)

        @block.scalar
        def _(act):
            for i, v in enumerate((A["w_cq"], A["w_q"], A["w_c"])):
                act.dma_start(w[:, i:i + 1], column(v)).then_inc(s["w_in"], 16)
            for i, v in enumerate((A["b_c"], A["b_q"], A["b_cq"])):
                act.dma_start(bs[:, i:i + 1], v.partition_broadcast(P)).then_inc(s["w_in"], 16)
            act.dma_start(wl[:, :, :], A["w_l"].rearrange("o (k i) -> o k i", k=4)).then_inc(s["w_in"], 16)
            act.dma_start(bl[:, :], A["b_l"].partition_broadcast(P)).then_inc(s["bl_in"], 16)
            norm_sqrt(act, ns, 0, TOKEN_TILES, 1)
            for i in range(2):
                act.wait_ge(s["transposed"], i + 1)
                act.activation(c_t[:, i * BANK:(i + 1) * BANK], B[i][:, :], ACT.Copy).then_inc(s["copied"], 1)
            act.wait_ge(s["m_ready"], 1)
            act.activation(m_h[:, :], m_t[:, :], ACT.Copy).then_inc(s["m_high"], 1)
            act.wait_ge(s["ctx_in"], 16)
            act.wait_ge(s["tail_in"], 16)
            act.activation(ctx_h[0:TAIL, CTX_TILES, :], tail[:, :], ACT.Copy).then_inc(s["rows_high"], 1)
            for k in range(QC):
                act.wait_ge(s["q_transposed"], k + 1)
                act.activation(q_h[:, k * BANK:k * BANK + width(k)], B[2 + k % 4][:, 0:width(k)], ACT.Copy)\
                   .then_inc(s["q_high"], 1)
                t = slice(4 * k, min(4 * k + 4, CTX_TILES))
                act.activation(ctx_h[:, t, :], ctx[:, t, :], ACT.Copy).then_inc(s["rows_high"], 1)
            act.wait_ge(s["wl_transposed"], 1)
            act.activation(wl_t[:, :, :].rearrange("p k o -> p (k o)"), B[6][:, :], ACT.Copy).then_inc(s["wl_copied"], 1)

            def exponents(i, p):
                act.wait_ge(s["max_ready"], i + 1)
                x = scores[:, i % 2, 2 * p * BANK:min(2 * (p + 1) * BANK, CONTEXT)]
                act.activation(x, x, ACT.Exp, bias=neg_top[:, i:i + 1], accum_out=den_parts[:, i, p:p + 1])\
                   .then_inc(s["exponents"], 1)

            exponents(0, 0)
            for i in range(TOKEN_TILES):
                for k in range(QC):
                    if k % 2 == 0 and k // 2 + 1 < PIECES:
                        exponents(i, k // 2 + 1)
                    if k == QC - 1 and i + 1 < TOKEN_TILES:
                        exponents(i + 1, 0)
                    act.wait_ge(s["probs_t"], i * QC + k + 1)
                    if i * QC + k >= NPT:
                        act.wait_ge(s["applied"], i * QC + k - NPT + 1)
                    x = (i * QC + k) % NPT
                    for lo, hi, n in spans(k):
                        last = act.activation(pt_h[0:n, x, lo:hi], B[3 + (i * QC + k) % 3][0:n, lo:hi], ACT.Copy)
                    last.then_inc(s["probs_high"], 1)
            act.wait_ge(s["spread_read"], 1)
            act.activation(b_att[:, :], level[:, :], ACT.Exp, bias=neg_all_max[:, 0:1]).then_inc(s["weights_ready"], 1)
            for i in range(2):
                act.wait_ge(s["c2q_transposed"], i + 1)
                act.activation(c2q_t[:, i * BANK:(i + 1) * BANK], B[i][:, :], ACT.Copy).then_inc(s["c2q_copied"], 1)

        @block.vector
        def _(dve):
            steps = Steps(dve, s["vec"])
            for t in range(TOKEN_TILES):
                last = dve.bn_stats(ns.stats[:, t, :], X[:, t, :])
            steps.link(last)
            norm_moments(dve, steps, ns, 0, TOKEN_TILES)
            norm_rstd(dve, steps, ns, 0, TOKEN_TILES, 1)
            for t in range(TOKEN_TILES):
                normalize(dve, c[:, t, :], X[:, t, :], ns, t).then_inc(s["normalized"], 1)
            dve.wait_ge(s["w_in"], 16 * 7)
            steps.done(dve.tensor_tensor(bs[:, 3:4], bs[:, 0:1], bs[:, 1:2], op=ALU.add))
            dve.wait_ge(steps.sem, steps.count)
            steps.link(dve.tensor_tensor(bs[:, 3:4], bs[:, 3:4], bs[:, 2:3], op=ALU.add))
            dve.wait_ge(s["copied"], 2)
            dve.tensor_scalar(m_t[:, :], c_t[:, :], w[:, 0:1], w[:, 1:2], ALU.mult, ALU.add).then_inc(s["m_ready"], 1)
            dve.wait_ge(s["m_high"], 1)
            dve.tensor_tensor(m_l[:, :], m_t[:, :], m_h[:, :], op=ALU.subtract).then_inc(s["m_split"], 1)
            dve.wait_ge(s["rows_high"], 1)
            dve.tensor_tensor(ctx_l[0:TAIL, CTX_TILES, :], tail[:, :], ctx_h[0:TAIL, CTX_TILES, :], op=ALU.subtract)\
               .then_inc(s["rows_split"], 1)
            for k in range(QC):
                dve.wait_ge(s["q_high"], k + 1)
                r = slice(k * BANK, k * BANK + width(k))
                dve.tensor_tensor(q_l[:, r], B[2 + k % 4][:, 0:width(k)], q_h[:, r], op=ALU.subtract)\
                   .then_inc(s["q_split"], 1)
                dve.wait_ge(s["rows_high"], k + 2)
                t = slice(4 * k, min(4 * k + 4, CTX_TILES))
                dve.tensor_tensor(ctx_l[:, t, :], ctx[:, t, :], ctx_h[:, t, :], op=ALU.subtract)\
                   .then_inc(s["rows_split"], 1)
            dve.wait_ge(s["level_done"], 1)
            steps.link(dve.tensor_scalar(level[:, :], B[7][:, 0:TOKEN_TILES], bs[:, 3:4], None, ALU.add))

            def store_chunk(i, k):
                x = i * QC + k
                dve.wait_ge(s["scored"], x + 1)
                if k == 0 and i >= 2:
                    dve.wait_ge(s["probs_t"], (i - 1) * QC)
                dve.tensor_scalar(scores[:, i % 2, k * BANK:k * BANK + width(k)], B[x % 3][:, 0:width(k)], 0.0, None,
                                  ALU.add, ALU.max, accum_out=chunk_max[:, k:k + 1]).then_inc(s["stored"], 1)

            def tile_max(i):
                dve.wait_ge(s["stored"], (i + 1) * QC)
                steps.link(dve.tensor_reduce(top[:, i:i + 1], chunk_max[:, :], axis=AX.X, op=ALU.max))
                dve.tensor_scalar(neg_top[:, i:i + 1], top[:, i:i + 1], -1.0, None, ALU.mult).then_inc(s["max_ready"], 1)

            def split_chunk(i, k):
                x = i * QC + k
                dve.wait_ge(s["probs_high"], x + 1)
                for lo, hi, n in spans(k):
                    last = dve.tensor_tensor(pt_l[0:n, x % NPT, lo:hi], B[3 + x % 3][0:n, lo:hi],
                                             pt_h[0:n, x % NPT, lo:hi], op=ALU.subtract)
                last.then_inc(s["probs_split"], 1)

            def finish_tile(i):
                dve.wait_ge(s["applied"], (i + 1) * QC)
                steps.link(dve.tensor_reduce(den[:, i:i + 1], den_parts[:, i, :], axis=AX.X, op=ALU.add))
                steps.link(dve.reciprocal(rden[:, i:i + 1], den[:, i:i + 1]))
                dve.tensor_scalar(c2q[:, i, :], B[6 + i % 2][:, 0:D], rden[:, i:i + 1], None, ALU.mult)\
                   .then_inc(s["applied_read"], 1)

            for k in range(QC):
                store_chunk(0, k)
            tile_max(0)
            for i in range(TOKEN_TILES):
                for k in range(QC):
                    if i + 1 < TOKEN_TILES:
                        for n in scored_in(k):
                            store_chunk(i + 1, n)
                        if k == SCORED_BY:
                            tile_max(i + 1)
                    split_chunk(i, k)
                    if k == APPLY_LAG and i:
                        finish_tile(i - 1)
            finish_tile(TOKEN_TILES - 1)
            steps.link(dve.tensor_tensor(level[:, :], level[:, :], top[:, :], op=ALU.add))
            dve.tensor_reduce(level_max[:, :], level[:, :], axis=AX.X, op=ALU.max).then_inc(s["level_ready"], 1)
            dve.wait_ge(s["row_ready"], 1)
            dve.tensor_reduce(one_max[:, :], B[4][0:1, 0:P], axis=AX.X, op=ALU.max).then_inc(s["one_ready"], 1)
            dve.wait_ge(s["spread"], 1)
            dve.tensor_scalar(neg_all_max[:, :], B[5][:, 0:1], -1.0, None, ALU.mult).then_inc(s["spread_read"], 1)
            dve.wait_ge(s["summed"], 1)
            steps.link(dve.reciprocal(rsum[:, :], B[4][:, 0:1]))
            steps.link(dve.tensor_scalar(q2c[:, :], B[5][:, 0:1], rsum[:, 0:1], None, ALU.mult))
            steps.done(dve.tensor_scalar(back_t[:, :], c_t[:, :], q2c[:, 0:1], None, ALU.mult))
            dve.wait_ge(s["c2q_copied"], 2)
            dve.tensor_tensor(mixed_t[:, :], c_t[:, :], c2q_t[:, :], op=ALU.mult).then_inc(s["factors"], 1)
            dve.wait_ge(s["bl_in"], 16)
            for i in range(2):
                for t in range(4 * i, 4 * i + 4):
                    last = dve.tensor_tensor(X[:, t, :], X[:, t, :], bl[:, :], op=ALU.add)
            steps.link(last)
            for i in range(2):
                dve.wait_ge(s["projected"], i + 1)
                x = X[:, 4 * i:4 * i + 4, :]
                dve.tensor_tensor(x, B[2 + i][:, :].rearrange("p (t d) -> p t d", d=D), x, op=ALU.add)\
                   .then_inc(s["added"], 1)

        @block.tensor
        def _(pe):
            for t in range(TOKEN_TILES):
                pe.wait_ge(s["normalized"], t + 1)
                last = pe.transpose(B[t // 4][:, (t % 4) * P:(t % 4 + 1) * P], c[:, t, :], ident[:, :])
                if t % 4 == 3:
                    last.then_inc(s["transposed"], 1)
            pe.wait_ge(s["w_in"], 16 * 7)
            for k in range(4):
                last = pe.transpose(B[6][:, k * P:(k + 1) * P], wl[:, k, :], ident[:, :])
            last.then_inc(s["wl_transposed"], 1)
            pe.wait_ge(s["copied"], 2)
            for t in range(TOKEN_TILES):
                last = pe.matmul(B[7][:, t:t + 1], c_t[:, t * P:(t + 1) * P], w[:, 2:3], start=True, stop=True)
            last.then_inc(s["level_done"], 1)
            pe.wait_ge(s["ctx_in"], 16)
            pe.wait_ge(s["tail_in"], 16)
            for k in range(QC):
                if k >= 4:
                    pe.wait_ge(s["q_split"], k - 3)
                for t in tiles_of(k):
                    n = rows(t)
                    src = ctx[:, t, :] if t < CTX_TILES else tail[:, :]
                    last = pe.transpose(B[2 + k % 4][:, (t % 4) * P:(t % 4) * P + n], src, ident[0:n, 0:n])
                last.then_inc(s["q_transposed"], 1)
            pe.wait_ge(s["m_split"], 1)
            pe.wait_ge(s["q_split"], QC)
            pe.wait_ge(s["rows_split"], QC + 1)
            pe.wait_ge(s["wl_copied"], 1)

            def score(i, k):
                x = i * QC + k
                if x >= 3:
                    pe.wait_ge(s["stored"], x - 2)
                ch, cl = (m[:, i * P:(i + 1) * P] for m in (m_h, m_l))
                r = slice(k * BANK, k * BANK + width(k))
                o = B[x % 3][:, 0:width(k)]
                pe.matmul(o, ch, q_h[:, r], start=True, stop=False)
                pe.matmul(o, ch, q_l[:, r], start=False, stop=False)
                pe.matmul(o, cl, q_h[:, r], start=False, stop=True).then_inc(s["scored"], 1)

            def transpose(i, k):
                x = i * QC + k
                if k % 2 == 0:
                    pe.wait_ge(s["exponents"], i * PIECES + k // 2 + 1)
                if x >= 3:
                    pe.wait_ge(s["probs_split"], x - 2)
                for t in tiles_of(k):
                    n = rows(t)
                    last = pe.transpose(B[3 + x % 3][0:n, (t % 4) * P:(t % 4 + 1) * P],
                                        scores[:, i % 2, t * P:t * P + n], ident[:, :])
                last.then_inc(s["probs_t"], 1)

            def apply(i, k):
                x = i * QC + k
                if k == 0 and i >= 2:
                    pe.wait_ge(s["applied_read"], i - 1)
                pe.wait_ge(s["probs_split"], x + 1)
                for t in tiles_of(k):
                    n = rows(t)
                    col = slice((t % 4) * P, (t % 4 + 1) * P)
                    ph, pl = pt_h[0:n, x % NPT, col], pt_l[0:n, x % NPT, col]
                    o = B[6 + i % 2][:, 0:D]
                    pe.matmul(o, ph, ctx_h[0:n, t, :], start=t == 0, stop=False)
                    pe.matmul(o, ph, ctx_l[0:n, t, :], start=False, stop=False)
                    last = pe.matmul(o, pl, ctx_h[0:n, t, :], start=False, stop=t == CTX_TILES)
                last.then_inc(s["applied"], 1)

            for k in range(QC):
                score(0, k)
            for x in range(TOKEN_TILES * QC + APPLY_LAG):
                i, k = divmod(x, QC)
                if i + 1 < TOKEN_TILES:
                    for n in scored_in(k):
                        score(i + 1, n)
                if i < TOKEN_TILES:
                    transpose(i, k)
                if x >= APPLY_LAG:
                    apply(*divmod(x - APPLY_LAG, QC))
            pe.wait_ge(s["level_ready"], 1)
            pe.wait_ge(s["ready_ones"], 1)
            pe.transpose(B[4][0:1, 0:P], level_max[:, :], ident[:, :]).then_inc(s["row_ready"], 1)
            pe.wait_ge(s["one_ready"], 1)
            pe.matmul(B[5][:, 0:1], ones[0:1, :], one_max[:, :], start=True, stop=True).then_inc(s["spread"], 1)
            pe.wait_ge(s["applied_read"], TOKEN_TILES)
            for t in range(TOKEN_TILES):
                last = pe.transpose(B[t // 4][:, (t % 4) * P:(t % 4 + 1) * P], c2q[:, t, :], ident[:, :])
                if t % 4 == 3:
                    last.then_inc(s["c2q_transposed"], 1)
            pe.wait_ge(s["weights_ready"], 1)
            for t in range(TOKEN_TILES):
                pe.matmul(B[4][:, 0:1], ones[:, :], b_att[:, t:t + 1], start=t == 0, stop=t == TOKEN_TILES - 1)
            for t in range(TOKEN_TILES):
                last = pe.matmul(B[5][:, 0:1], c[:, t, :], b_att[:, t:t + 1], start=t == 0, stop=t == TOKEN_TILES - 1)
            last.then_inc(s["summed"], 1)
            pe.wait_ge(s["factors"], 1)
            for t in range(TOKEN_TILES):
                for n, part in enumerate((c_t, c2q_t, mixed_t, back_t)):
                    last = pe.matmul(B[2 + t // 4][:, (t % 4) * D:(t % 4 + 1) * D], part[:, t * P:(t + 1) * P],
                                     wl_t[:, n, :], start=n == 0, stop=n == 3)
                if t % 4 == 3:
                    last.then_inc(s["projected"], 1)


class Persistent:

    def __init__(self, sc):
        self.whole = sc
        self.X = sc.sb("X", [P, TOKEN_TILES, D])
        self.ident = sc.sb("ident", [P, P])
        self.banks = sc.ps("banks", [P, 8, BANK])


def for_attention(pers, sc):
    pers.kvh = sc.sb("kvh", [P, KEYS], F16)
    pers.kvl = sc.sb("kvl", [P, KEYS], F16)
    pers.wk_h = sc.sb("wk_h", [P, HEADS, 2, DH], F16)
    pers.wk_l = sc.sb("wk_l", [P, HEADS, 2, DH], F16)
    pers.wq_h = sc.sb("wq_h", [P, HEADS, 2, DH], F16)
    pers.wq_l = sc.sb("wq_l", [P, HEADS, 2, DH], F16)
    pers.wv_h = sc.sb("wv_h", [P, HEADS * DH], F16)
    pers.wv_l = sc.sb("wv_l", [P, HEADS * DH], F16)
    pers.att = sc.sb("att", [P, TOKEN_TILES, HEADS * DH])


def build(nc, a, out):
    attention = dict(x=a["x"], ctx=a["ctx_1024"], ln_m_g=a["L0_xattn_ln_m_g"], ln_m_b=a["L0_xattn_ln_m_b"],
                     ln_l_g=a["L0_xattn_ln_l_g"], ln_l_b=a["L0_xattn_ln_l_b"], wq=a["L0_xattn_Wq"],
                     wkv=a["L0_xattn_Wkv"], wout=a["L0_xattn_Wout"])
    experts0 = dict(control=a["L0_ffn_controller"], up=a["L0_ffn_f1"], up_bias=a["L0_ffn_bias"], down=a["L0_ffn_f2"])
    cross = dict(ctx=a["ctx_1024"], w_cq=a["L1_xattn_w_cq"], b_cq=a["L1_xattn_b_cq"], w_c=a["L1_xattn_w_c"],
                 b_c=a["L1_xattn_b_c"], w_q=a["L1_xattn_w_q"], b_q=a["L1_xattn_b_q"], w_l=a["L1_xattn_W_l"],
                 b_l=a["L1_xattn_b_l"])
    experts1 = dict(control=a["L1_ffn_Wc"], control_bias=a["L1_ffn_bc"], up=a["L1_ffn_W1"], up_bias=a["L1_ffn_b1"],
                    down=a["L1_ffn_W2"], down_bias=a["L1_ffn_b2"])
    whole = Scope(nc, "all")
    with whole:
        pers = Persistent(whole)
        shared = Scope(nc, "shared")
        with shared:
            for_attention(pers, shared)
            stage_prepare(nc, pers, attention)
            stage_attention(nc, pers, attention)
            stage_attention_out(nc, pers, attention)
        whole.clear_semaphores()
        stage_experts(nc, pers, experts0, "experts0", 0)
        stage_cross(nc, pers, cross)
        stage_experts(nc, pers, experts1, "experts1", 1, out)


_INS = ["x", "ctx_1024", "L0_xattn_ln_m_g", "L0_xattn_ln_m_b", "L0_xattn_ln_l_g", "L0_xattn_ln_l_b", "L0_xattn_Wq",
        "L0_xattn_Wkv", "L0_xattn_Wout", "L0_ffn_controller", "L0_ffn_f1", "L0_ffn_bias", "L0_ffn_f2",
        "L1_xattn_w_cq", "L1_xattn_b_cq", "L1_xattn_w_c", "L1_xattn_b_c", "L1_xattn_w_q", "L1_xattn_b_q",
        "L1_xattn_W_l", "L1_xattn_b_l", "L1_ffn_Wc", "L1_ffn_bc", "L1_ffn_W1", "L1_ffn_b1", "L1_ffn_W2", "L1_ffn_b2"]


def kernel(**inputs):
    import numpy as _np
    import concourse.bacc as _bacc
    from concourse import mybir as _mybir
    from concourse.bass_utils import run_bass_kernel_spmd as _run

    nc = _bacc.Bacc("TRN2", target_bir_lowering=False, num_devices=1)
    arrays, args = {}, {}
    for name in _INS:
        a = _np.ascontiguousarray(inputs[name])
        if a.ndim == 0:
            a = a.reshape(1)
        arrays[f"in_{name}"] = a
        args[name] = nc.dram_tensor(f"in_{name}", a.shape, _mybir.dt.from_np(a.dtype), kind="ExternalInput").ap()
    out = nc.dram_tensor("out", (1, TOKENS, D), F32, kind="ExternalOutput").ap()
    build(nc, args, out)
    r = _run(nc, [arrays], core_ids=[0])
    return r.results[0]["out"]
```

```python
from contextlib import ExitStack

import concourse.bass as bass
from concourse import mybir

F32 = mybir.dt.float32
F16 = mybir.dt.float16
BF16 = mybir.dt.bfloat16
ALU = mybir.AluOpType
ACT = mybir.ActivationFunctionType
AX = mybir.AxisListType

P = 128
TOKENS, CONTEXT, D = 1024, 6404, 128
TOKEN_TILES = TOKENS // P
CTX_TILES = CONTEXT // P
CTX_ROWS = CTX_TILES * P
TAIL = CONTEXT - CTX_ROWS
EPS = 1e-5

HEADS, DH = 16, 64
INNER = HEADS * DH
KEYS = CONTEXT + TOKENS
FULL_TILES = CTX_TILES + TOKEN_TILES
KEY_TILES = FULL_TILES + 1
KEY_COLS = KEY_TILES * P
LATENT_COL = CTX_TILES * P
BANK = 512
K_CHUNKS = -(-KEYS // BANK)
V_GROUPS = -(-KEY_TILES // 8)
VCOLS = 2 * DH + 1
BODY = 14
BODIES = FULL_TILES // BODY
LOOP_TILES = BODY * BODIES
MAX_CHUNKS = 7
MAX_SLOTS = TOKEN_TILES * MAX_CHUNKS
REST_COL = MAX_CHUNKS * 2 * BANK
REST = KEYS - REST_COL
REST_STEPS = TOKEN_TILES // 2
SCALE = DH ** -0.5
LIFT = 6.931471805599453 / SCALE

EXPERTS, SETS, ESIZE = 32, 4, 32
ES = EXPERTS * SETS
GROUP = EXPERTS
GROUPS = TOKENS // GROUP
TIE_STEP = 1e-6 / (GROUP - 1)


class Steps:

    def __init__(self, engine, sem):
        self.engine, self.sem, self.count = engine, sem, 0

    def done(self, instruction):
        instruction.then_inc(self.sem, 1)
        self.count += 1

    def link(self, instruction):
        self.done(instruction)
        self.engine.wait_ge(self.sem, self.count)


class Scope(ExitStack):

    def __init__(self, nc, name, whole=None):
        super().__init__()
        self.nc, self.name = nc, name
        self.semaphores = whole.semaphores if whole else []

    def sb(self, name, shape, dtype=F32):
        return self.enter_context(self.nc.sbuf_tensor(f"{self.name}_{name}", shape, dtype))

    def ps(self, name, shape, dtype=F32):
        return self.enter_context(self.nc.psum_tensor(f"{self.name}_{name}", shape, dtype))

    def sem(self, name):
        sem = self.nc.alloc_semaphore(name=f"{self.name}_{name}")
        self.semaphores.append(sem)
        return sem

    def clear_semaphores(self):
        self.nc.all_engine_barrier()
        self.nc.clear_and_free_semaphores(self.semaphores)
        self.nc.all_engine_barrier()
        self.semaphores.clear()


class NormState:

    def __init__(self, sc, name, tiles):
        self.stats = sc.sb(name + "_stats", [P, tiles, 6])
        self.a = sc.sb(name + "_a", [P, tiles])
        self.b = sc.sb(name + "_b", [P, tiles])
        self.var = sc.sb(name + "_var", [P, tiles])
        self.mean = sc.sb(name + "_mean", [P, tiles])
        self.std = sc.sb(name + "_std", [P, tiles])
        self.rstd = sc.sb(name + "_rstd", [P, tiles])
        self.var_ready = sc.sem(name + "_var_ready")
        self.std_ready = sc.sem(name + "_std_ready")


def norm_moments(dve, steps, ns, lo, hi, n=P):
    st = ns.stats
    a, b, var, mean = (t[0:n, lo:hi] for t in (ns.a, ns.b, ns.var, ns.mean))
    steps.done(dve.tensor_tensor(a, st[0:n, lo:hi, 1], st[0:n, lo:hi, 4], op=ALU.add))
    steps.done(dve.tensor_tensor(b, st[0:n, lo:hi, 1], st[0:n, lo:hi, 4], op=ALU.subtract))
    steps.link(dve.tensor_tensor(var, st[0:n, lo:hi, 2], st[0:n, lo:hi, 5], op=ALU.add))
    steps.done(dve.tensor_scalar(mean, a, 0.5, None, ALU.mult))
    steps.done(dve.tensor_scalar(var, var, 1.0 / D, EPS, ALU.mult, ALU.add))
    steps.link(dve.tensor_tensor(b, b, b, op=ALU.mult))
    dve.scalar_tensor_tensor(var, b, 0.25, var, ALU.mult, ALU.add).then_inc(ns.var_ready, 1)


def norm_rstd(dve, steps, ns, lo, hi, turn, n=P):
    var, std, r, a = (t[0:n, lo:hi] for t in (ns.var, ns.std, ns.rstd, ns.a))
    dve.wait_ge(ns.std_ready, turn)
    steps.link(dve.reciprocal(r, std))
    steps.link(dve.tensor_tensor(a, r, r, op=ALU.mult))
    steps.link(dve.tensor_tensor(a, a, var, op=ALU.mult))
    steps.link(dve.tensor_scalar(a, a, -0.5, 1.5, ALU.mult, ALU.add))
    steps.link(dve.tensor_tensor(r, r, a, op=ALU.mult))


def norm_sqrt(act, ns, lo, hi, turn, n=P):
    act.wait_ge(ns.var_ready, turn)
    act.activation(ns.std[0:n, lo:hi], ns.var[0:n, lo:hi], ACT.Sqrt).then_inc(ns.std_ready, 1)


def normalize(dve, out, in_, ns, t, n=P):
    return dve.tensor_scalar(out, in_, ns.mean[0:n, t:t + 1], ns.rstd[0:n, t:t + 1], ALU.subtract, ALU.mult)


def column(vector):
    return vector.rearrange("(p one) -> p one", one=1)


def spread_columns(a, n):
    return a.rearrange("p (k one) -> p k one", one=1).to_broadcast([a.shape[0], a.shape[1], n])


def stage_prepare(nc, pers, A):
    sc = Scope(nc, "prep", pers.whole)
    with sc:
        ctx = sc.sb("ctx", [P, CTX_TILES, D])
        tail = sc.sb("tail", [TAIL, D])
        lat = sc.sb("lat", [P, TOKEN_TILES, D])
        wq = sc.sb("wq", [P, HEADS * DH])
        wkv = sc.sb("wkv", [P, 2 * HEADS * DH])
        gains = sc.sb("gains", [P, 4])
        NF = 4
        full = sc.sb("full", [P, NF, BANK])
        T = [pers.banks[:, n, :] for n in range(NF)]
        nx = NormState(sc, "nx", TOKEN_TILES)
        nl = NormState(sc, "nl", TOKEN_TILES)
        nk = NormState(sc, "nk", CTX_TILES + 1)
        x_in, w_in, g_in, tail_in = (sc.sem(n) for n in ("x_in", "w_in", "g_in", "tail_in"))
        CL = 5
        PER = CTX_TILES // CL
        ctx_in = [sc.sem(f"ctx_in{n}") for n in range(CL)]
        zeroed, ident_ready = sc.sem("zeroed"), sc.sem("ident_ready")
        vec, tile_ready, transposed = sc.sem("vec"), sc.sem("tile_ready"), sc.sem("transposed")
        full_ready, high_ready, low_ready = sc.sem("full_ready"), sc.sem("high_ready"), sc.sem("low_ready")
        w_high = sc.sem("w_high")
        w_done = sc.sem("w_done")
        X, kvh, kvl, ident = pers.X, pers.kvh, pers.kvl, pers.ident

        def tiles_of(c):
            return [t for t in range(4 * c, min(4 * c + 4, KEY_TILES))]

        def width(c):
            return min(BANK, KEYS - c * BANK)

        block = sc.enter_context(nc.Block())

        @block.sync
        def _(sp):
            sp.dma_start(X[:, :, :], A["x"][0].rearrange("(t p) d -> p t d", p=P)).then_inc(x_in, 16)
            body = A["ctx"][0, 0:CTX_ROWS, :].rearrange("(p t) d -> p t d", p=P)
            for n in range(CL):
                sp.dma_start(ctx[:, n * PER:(n + 1) * PER, :], body[:, n * PER:(n + 1) * PER, :])\
                  .then_inc(ctx_in[n], 16)
            sp.dma_start(tail[:, :], A["ctx"][0, CTX_ROWS:CONTEXT, :]).then_inc(tail_in, 16)

        @block.scalar
        def _(act):
            for n, v in enumerate((A["ln_m_g"], A["ln_m_b"], A["ln_l_g"], A["ln_l_b"])):
                act.dma_start(gains[:, n:n + 1], column(v)).then_inc(g_in, 16)
            act.dma_start(wkv[:, :], A["wkv"]).then_inc(w_in, 16)
            act.dma_start(wq[:, :], A["wq"]).then_inc(w_in, 16)
            norm_sqrt(act, nx, 0, TOKEN_TILES, 1)
            norm_sqrt(act, nl, 0, TOKEN_TILES, 1)
            for n in range(CL):
                norm_sqrt(act, nk, n * PER, (n + 1) * PER, n + 1)
                if n == CL // 2:
                    act.wait_ge(w_in, 32)
                    for r in range(2):
                        act.activation(pers.wk_h[:, :, r, :], wkv[:, 0:INNER].rearrange("p (h d) -> p h d", d=DH), ACT.Copy)\
                           .then_inc(w_high, 1)
                        act.activation(pers.wq_h[:, :, r, :], wq[:, :].rearrange("p (h d) -> p h d", d=DH), ACT.Copy)\
                           .then_inc(w_high, 1)
                    act.activation(pers.wv_h[:, :], wkv[:, INNER:2 * INNER], ACT.Copy).then_inc(w_high, 1)
            norm_sqrt(act, nk, CTX_TILES, CTX_TILES + 1, CL + 1, TAIL)
            act.wait_ge(g_in, 64)
            for c in range(K_CHUNKS):
                act.wait_ge(transposed, c + 1)
                if c >= NF:
                    act.wait_ge(low_ready, c - NF + 1)
                w = width(c)
                parts = []
                for t in tiles_of(c):
                    n = TAIL if t == FULL_TILES else P
                    kind = 2 if CTX_TILES <= t < FULL_TILES else 0
                    o = (t % 4) * P
                    if parts and parts[-1][2] == kind:
                        parts[-1][1] = o + n
                    else:
                        parts.append([o, o + n, kind])
                for o0, o1, kind in parts:
                    g, b = gains[:, kind:kind + 1], gains[:, kind + 1:kind + 2]
                    last = act.activation(full[:, c % NF, o0:o1], T[c % NF][:, o0:o1], ACT.Identity, bias=b, scale=g)
                    if o1 == w:
                        last.then_inc(full_ready, 1)
                    last = act.activation(kvh[:, c * BANK + o0:c * BANK + o1], T[c % NF][:, o0:o1], ACT.Identity,
                                          bias=b, scale=g)
                    if o1 == w:
                        last.then_inc(high_ready, 1)

        @block.gpsimd
        def _(pool):
            pool.memset(ident[:, :], 0.0).then_inc(zeroed, 1)
            pool.wait_ge(zeroed, 1)
            pool.affine_select(out=ident[:, :], in_=ident[:, :], compare_op=ALU.not_equal, fill=1.0, base=0,
                               pattern=[[-1, P]], channel_multiplier=1).then_inc(ident_ready, 1)
            pool.wait_ge(w_high, 5)
            for r in range(2):
                pool.tensor_tensor(pers.wk_l[:, :, r, :], wkv[:, 0:INNER].rearrange("p (h d) -> p h d", d=DH),
                                   pers.wk_h[:, :, r, :], op=ALU.subtract).then_inc(w_done, 1)
                pool.tensor_tensor(pers.wq_l[:, :, r, :], wq[:, :].rearrange("p (h d) -> p h d", d=DH),
                                   pers.wq_h[:, :, r, :], op=ALU.subtract).then_inc(w_done, 1)
            pool.tensor_tensor(pers.wv_l[:, :], wkv[:, INNER:2 * INNER], pers.wv_h[:, :], op=ALU.subtract)\
                .then_inc(w_done, 1)

        @block.vector
        def _(dve):
            steps = Steps(dve, vec)
            dve.wait_ge(x_in, 16)
            for t in range(TOKEN_TILES):
                last = dve.bn_stats(nx.stats[:, t, :], X[:, t, :])
            steps.link(last)
            norm_moments(dve, steps, nx, 0, TOKEN_TILES)
            norm_rstd(dve, steps, nx, 0, TOKEN_TILES, 1)
            for t in range(TOKEN_TILES):
                last = normalize(dve, lat[:, t, :], X[:, t, :], nx, t)
            steps.link(last)
            for t in range(TOKEN_TILES):
                last = dve.bn_stats(nl.stats[:, t, :], lat[:, t, :])
            steps.link(last)
            norm_moments(dve, steps, nl, 0, TOKEN_TILES)
            norm_rstd(dve, steps, nl, 0, TOKEN_TILES, 1)
            for n in range(CL):
                dve.wait_ge(ctx_in[n], 16)
                for t in range(n * PER, (n + 1) * PER):
                    last = dve.bn_stats(nk.stats[:, t, :], ctx[:, t, :])
                steps.link(last)
                norm_moments(dve, steps, nk, n * PER, (n + 1) * PER)
            dve.wait_ge(tail_in, 16)
            steps.link(dve.bn_stats(nk.stats[0:TAIL, CTX_TILES, :], tail[:, :]))
            norm_moments(dve, steps, nk, CTX_TILES, CTX_TILES + 1, TAIL)
            norm_rstd(dve, steps, nk, 0, CTX_TILES, CL)
            norm_rstd(dve, steps, nk, CTX_TILES, CTX_TILES + 1, CL + 1, TAIL)

            def low_parts(c):
                dve.wait_ge(full_ready, c + 1)
                dve.wait_ge(high_ready, c + 1)
                k = slice(c * BANK, c * BANK + width(c))
                dve.tensor_tensor(kvl[:, k], full[:, c % NF, 0:width(c)], kvh[:, k], op=ALU.subtract)\
                   .then_inc(low_ready, 1)

            for c in range(K_CHUNKS):
                for t in tiles_of(c):
                    if t < CTX_TILES:
                        i = normalize(dve, ctx[:, t, :], ctx[:, t, :], nk, t)
                    elif t < FULL_TILES:
                        i = normalize(dve, lat[:, t - CTX_TILES, :], lat[:, t - CTX_TILES, :], nl, t - CTX_TILES)
                    else:
                        i = normalize(dve, tail[:, :], tail[:, :], nk, CTX_TILES, TAIL)
                    i.then_inc(tile_ready, 1)
                if c >= 2:
                    low_parts(c - 2)
            low_parts(K_CHUNKS - 2)
            low_parts(K_CHUNKS - 1)

        @block.tensor
        def _(pe):
            pe.wait_ge(ident_ready, 1)
            for c in range(K_CHUNKS):
                if c >= NF:
                    pe.wait_ge(high_ready, c - NF + 1)
                for t in tiles_of(c):
                    pe.wait_ge(tile_ready, t + 1)
                    n = TAIL if t == FULL_TILES else P
                    src = ctx[:, t, :] if t < CTX_TILES else lat[:, t - CTX_TILES, :] if t < FULL_TILES else tail[:, :]
                    last = pe.transpose(T[c % NF][:, (t % 4) * P:(t % 4) * P + n], src, ident[0:n, 0:n])
                last.then_inc(transposed, 1)


def stage_attention(nc, pers, A):
    sc = Scope(nc, "att", pers.whole)
    with sc:
        kc = sc.sb("kc", [P, 2, KEY_COLS], F16)
        kd = sc.sb("kd", [P, 2, KEY_COLS], F16)
        v = sc.sb("v", [P, 2, KEY_TILES, VCOLS], F16)
        qc = sc.sb("qc", [P, 2, TOKENS], F16)
        qd = sc.sb("qd", [P, 2, TOKENS], F16)
        prob = [sc.sb(f"prob{n}", [P, TOKENS]) for n in range(2)]
        prob_low = [sc.sb(f"prob_low{n}", [P, TOKENS], F16) for n in range(2)]
        scores16 = [sc.sb(f"scores16_{n}", [P, 2 * BANK], BF16) for n in range(2)]
        running = [sc.sb(f"running{n}", [P, 2 * BANK], BF16) for n in range(2)]
        loop_max = sc.sb("loop_max", [P, TOKEN_TILES])
        rest_max = sc.sb("rest_max", [P, TOKEN_TILES])
        top = sc.sb("top", [P, TOKEN_TILES])
        rden = sc.sb("rden", [P, TOKEN_TILES])
        zeros = sc.sb("zeros", [P, BANK], F16)
        warm = sc.sb("warm", [1, 1])
        S = [pers.banks[:, 2 * n:2 * n + 2, :].rearrange("p b q -> p (b q)") for n in range(2)]
        X = pers.banks[:, 4:6, :]
        O = pers.banks[:, 6:8, :]
        FIRST, SECOND, INNER_HEAD, AFTER_LAST = "first", "second", "inner", "after last"
        SLOT_BANKS = [X, pers.banks[:, 0:2, :]]
        names = ("k_projected k_high k_split v_projected v_high v_split q_projected q_high q_split constants filled "
                 "scored exp_done prob_split applied max_scored max_copied max_taken folded max_reduced rest_scored "
                 "rest_reduced top_ready top_spread top_placed inverted normalized").split()
        s = {n: sc.sem(n) for n in names}
        (k_projected, k_high, k_split, v_projected, v_high, v_split, q_projected, q_high, q_split, constants, filled,
         scored, exp_done, prob_split, applied, max_scored, max_copied, max_taken, folded, max_reduced, rest_scored,
         rest_reduced, top_ready, top_spread, top_placed, inverted, normalized) = (s[n] for n in names)
        kvh, kvl, ident, att = pers.kvh, pers.kvl, pers.ident, pers.att
        EXP0, NORM0, TAKEN0, REDUCED0 = 1, 1, 2, 2

        def dyn(i, size=1):
            return bass.ds(i, size)

        def kwidth(c):
            return min(BANK, KEYS - c * BANK)

        def bank(c):
            return S[1 - c % 4 // 2][:, (c % 2) * BANK:(c % 2) * BANK + kwidth(c)]

        def group(g):
            return list(range(8 * g, min(8 * g + 8, KEY_TILES)))

        def between_heads(kind):
            first, last = kind == FIRST, kind == AFTER_LAST
            after = kind in (INNER_HEAD, AFTER_LAST)

            def k(*chunks):
                return [] if last else [("k", c) for c in chunks]

            def if_after(what):
                return [(what, 0)] if after else []

            def if_max(*steps):
                return [] if first else list(steps)

            r = REST_STEPS - 1
            order = if_after("tail_split") + if_max(("rest_product", r - 1), ("rest", r - 1)) + if_after("fold") + k(0)
            order += if_max(("rest", r), ("finish", 0)) + k(1) + if_max(("rest_product", r))
            order += if_after("tail_high") + k(2) + if_after("tail_low") + k(3) + if_max(("top", 0)) + k(4, 5)
            order += if_after("norm")
            if not last:
                order += [("q", 0), ("q", 1)] + k(6, 7)
                for c in range(8, K_CHUNKS - 1):
                    order += k(c) + [("v", c - 8)]
                order += k(K_CHUNKS - 1) + [("v", g) for g in range(K_CHUNKS - 9, V_GROUPS)]
            return order

        block = sc.enter_context(nc.Block())

        @block.gpsimd
        def _(pool):
            pool.memset(kd[DH:P, :, :], 1.0 / DH).then_inc(filled, 1)
            pool.wait_ge(filled, 1)
            pool.memset(v[:, :, :, DH:DH + 1], 1.0).then_inc(filled, 1)

        @block.tensor
        def _(pe):
            def project_k(a, c, first):
                if c >= 4:
                    pe.wait_ge(k_split, a * K_CHUNKS + c - 3)
                elif not first:
                    pe.wait_ge(k_split, a * K_CHUNKS)
                    pe.wait_ge(exp_done, EXP0 + (a - 1) * KEY_TILES - (1 if c < 2 else 0))
                    pe.wait_ge(max_copied, a * MAX_SLOTS)
                r = kvh[:, c * BANK:c * BANK + kwidth(c)]
                rl = kvl[:, c * BANK:c * BANK + kwidth(c)]
                wh = pers.wk_h[:, dyn(a), :, :].rearrange("p a r d -> p (a r d)")
                wl = pers.wk_l[:, dyn(a), :, :].rearrange("p a r d -> p (a r d)")
                pe.matmul(bank(c), wh, r, start=True, stop=False)
                pe.matmul(bank(c), wh, rl, start=False, stop=False)
                pe.matmul(bank(c), wl, r, start=False, stop=True).then_inc(k_projected, 1)

            def project_v(a, g):
                if g >= 2:
                    pe.wait_ge(v_split, a * V_GROUPS + g - 1)
                else:
                    pe.wait_ge(q_split, a * 4 + 2 * g + 2)
                wh = pers.wv_h[:, dyn(a * DH, DH)]
                wl = pers.wv_l[:, dyn(a * DH, DH)]
                for t in group(g):
                    n = TAIL if t == FULL_TILES else P
                    o = X[0:n, g % 2, (t % 8) * DH:(t % 8 + 1) * DH]
                    th, tl = kvh[:, t * P:t * P + n], kvl[:, t * P:t * P + n]
                    pe.matmul(o, th, wh, start=True, stop=False)
                    pe.matmul(o, th, wl, start=False, stop=False)
                    last = pe.matmul(o, tl, wh, start=False, stop=True)
                last.then_inc(v_projected, 1)

            def project_q(a, i, first):
                if not first:
                    pe.wait_ge(top_placed, a)
                r = kvh[:, LATENT_COL + i * BANK:LATENT_COL + (i + 1) * BANK]
                rl = kvl[:, LATENT_COL + i * BANK:LATENT_COL + (i + 1) * BANK]
                wh = pers.wq_h[:, dyn(a), :, :].rearrange("p a r d -> p (a r d)")
                wl = pers.wq_l[:, dyn(a), :, :].rearrange("p a r d -> p (a r d)")
                pe.matmul(X[:, i, :], wh, r, start=True, stop=False)
                pe.matmul(X[:, i, :], wh, rl, start=False, stop=False)
                pe.matmul(X[:, i, :], wl, r, start=False, stop=True).then_inc(q_projected, 1)

            def project(a, kind):
                for what, n in between_heads(kind):
                    if what == "k":
                        project_k(a, n, kind == FIRST)
                    elif what == "rest_product":
                        rest_step(a - 1, n)
                    elif what == "top":
                        spread_top(a - 1)
                    elif what == "tail_high":
                        apply_high(a - 2, FULL_TILES, FULL_TILES, TAIL)
                    elif what == "tail_low":
                        apply_low(a - 2, FULL_TILES, FULL_TILES, TAIL)
                    elif what == "q":
                        project_q(a, n, kind == FIRST)
                    elif what == "v":
                        project_v(a, n)

            def max_slot(m, j, c, slot, ready, banks=X, lead=0):
                if ready:
                    pe.wait_ge(k_split, (m + 1) * K_CHUNKS)
                    pe.wait_ge(q_split, (m + 1) * 4)
                    pe.wait_ge(v_split, (m + 1) * V_GROUPS)
                else:
                    pe.wait_ge(max_copied, m * MAX_SLOTS + slot - lead)
                par = m % 2
                lhs = qc[:, dyn(par), dyn(j * P, P)].rearrange("p a q -> p (a q)")
                for i in range(2):
                    rhs = kc[:, dyn(par), (2 * c + i) * BANK:(2 * c + i + 1) * BANK].rearrange("p a q -> p (a q)")
                    last = pe.matmul(banks[:, i, :], lhs, rhs, start=True, stop=True)
                last.then_inc(max_scored, 1)

            def rest_step(m, r):
                if r == 0:
                    pe.wait_ge(max_copied, (m + 1) * MAX_SLOTS)
                else:
                    pe.wait_ge(rest_reduced, m * REST_STEPS + r)
                par = m % 2
                for i in range(2):
                    j = 2 * r + i
                    lhs = qc[:, dyn(par), j * P:(j + 1) * P].rearrange("p a q -> p (a q)")
                    rhs = kc[:, dyn(par), REST_COL:KEYS].rearrange("p a q -> p (a q)")
                    last = pe.matmul(X[:, i, 0:REST], lhs, rhs, start=True, stop=True)
                last.then_inc(rest_scored, 1)

            def spread_top(m):
                pe.wait_ge(top_ready, m + 1)
                for j in range(TOKEN_TILES):
                    o = X[DH:P, j // 4, (j % 4) * P:(j % 4 + 1) * P]
                    last = pe.matmul(o, top[:, j:j + 1].to_broadcast([P, DH]), ident[:, :], start=True, stop=True)
                last.then_inc(top_spread, 1)

            def score(b, t, tile, after_projection):
                if after_projection is None:
                    pe.wait_ge(exp_done, EXP0 + b * KEY_TILES + tile - 1)
                elif after_projection:
                    pe.wait_ge(k_split, (b + 2) * K_CHUNKS)
                else:
                    pe.wait_ge(exp_done, EXP0 + b * KEY_TILES)
                par = b % 2
                st = S[t % 2]
                for lhs, rhs, start in ((kc, qc, True), (kd, qd, False)):
                    w = lhs[:, dyn(par), dyn(tile * P, P)].rearrange("p a q -> p (a q)")
                    for i in range(2):
                        r = rhs[:, dyn(par), i * BANK:(i + 1) * BANK].rearrange("p a q -> p (a q)")
                        last = pe.matmul(st[:, i * BANK:(i + 1) * BANK], w, r, start=start, stop=not start)
                last.then_inc(scored, 1)

            def wait_on_zeros():
                pe.matmul(O[:, 0, 0:DH], zeros[:, 0:P], zeros[:, 0:DH], start=False, stop=False, skip_group_check=True)

            def apply_high(b, t, tile, n=P):
                par = b % 2
                high = v[0:n, dyn(par), dyn(tile), 0:DH + 1].rearrange("p a t c -> p (a t c)")
                low = v[0:n, dyn(par), dyn(tile), DH + 1:VCOLS].rearrange("p a t c -> p (a t c)")
                pe.wait_ge(exp_done, EXP0 + b * KEY_TILES + tile + 1)
                if n < P:
                    wait_on_zeros()
                for j in range(TOKEN_TILES):
                    w = prob[t % 2][0:n, :].bitcast(BF16)[:, 2 * j * P + 1:2 * (j + 1) * P:2]
                    o = (j % 4) * (DH + 1)
                    pe.matmul(O[:, j // 4, o:o + DH + 1], w, high, start=False, stop=False, skip_group_check=True)
                    pe.matmul(O[:, j // 4, o:o + DH], w, low, start=False, stop=False, skip_group_check=True)

            def apply_low(b, t, tile, n=P):
                high = v[0:n, dyn(b % 2), dyn(tile), 0:DH + 1].rearrange("p a t c -> p (a t c)")
                pe.wait_ge(prob_split, b * KEY_TILES + tile + 1)
                if n < P:
                    wait_on_zeros()
                for j in range(TOKEN_TILES):
                    w = prob_low[t % 2][0:n, j * P:(j + 1) * P]
                    o = (j % 4) * (DH + 1)
                    last = pe.matmul(O[:, j // 4, o:o + DH + 1], w, high, start=False, stop=True,
                                     skip_group_check=True)
                last.then_inc(applied, 1)

            def attend(b, with_max):
                m = b + 1
                pe.wait_ge(top_placed, b + 1)
                pe.wait_ge(normalized, NORM0 + b)
                for i in range(2):
                    pe.matmul(O[:, i, :], zeros[:, 0:P], zeros[:, :], start=True, stop=False, skip_group_check=True)
                score(b, 0, 0, with_max)
                score(b, 1, 1, with_max)
                pe.wait_ge(v_split, (b + 1) * V_GROUPS)

                def tile_step(t, tile, slot, ready):
                    apply_high(b, t, tile)
                    if with_max:
                        max_slot(m, slot[0], slot[1], slot[2], ready)
                        apply_low(b, t, tile)
                        score(b, t, tile + 2, None)
                    else:
                        score(b, t, tile + 2, None)
                        apply_low(b, t, tile)

                for u in range(BODY):
                    tile_step(u, u, (u // MAX_CHUNKS, u % MAX_CHUNKS, u), u == 0)
                with pe.Fori(1, BODIES) as jj:
                    for u in range(BODY):
                        tile_step(u, jj * BODY + u, (jj * 2 + u // MAX_CHUNKS, u % MAX_CHUNKS, jj * BODY + u), False)
                for t in range(LOOP_TILES, FULL_TILES if with_max else KEY_TILES):
                    n = TAIL if t == FULL_TILES else P
                    apply_high(b, t, t, n)
                    if with_max:
                        rest_step(m, t - LOOP_TILES)
                    apply_low(b, t, t, n)
                    if t + 2 < KEY_TILES:
                        score(b, t, t + 2, None)

            pe.wait_ge(constants, 3)
            project(0, FIRST)
            for u in range(BODY):
                max_slot(0, u // MAX_CHUNKS, u % MAX_CHUNKS, u, u < 2, SLOT_BANKS[u % 2], 1)
            with pe.Fori(1, BODIES) as jj:
                for u in range(BODY):
                    max_slot(0, jj * 2 + u // MAX_CHUNKS, u % MAX_CHUNKS, jj * BODY + u, False, SLOT_BANKS[u % 2], 1)
            for r in range(REST_STEPS - 2):
                rest_step(0, r)
            pe.wait_ge(filled, 2)
            project(1, SECOND)
            attend(0, True)
            with pe.Fori(1, HEADS - 1) as h:
                project(h + 1, INNER_HEAD)
                attend(h, True)
            project(HEADS, AFTER_LAST)
            attend(HEADS - 1, False)

        @block.scalar
        def _(act):
            def project(a, kind):
                par = a % 2
                for what, n in between_heads(kind):
                    if what == "k":
                        act.wait_ge(k_projected, a * K_CHUNKS + n + 1)
                        o = kc[:, dyn(par), n * BANK:n * BANK + kwidth(n)].rearrange("p a q -> p (a q)")
                        act.activation(o, bank(n), ACT.Copy).then_inc(k_high, 1)
                    elif what == "q":
                        act.wait_ge(q_projected, a * 2 + n + 1)
                        o = qc[:, dyn(par), n * BANK:(n + 1) * BANK].rearrange("p a q -> p (a q)")
                        act.activation(o, X[:, n, :], ACT.Copy).then_inc(q_high, 1)
                    elif what == "v":
                        copy_v(a, n)
                    elif what == "top":
                        place_top(a - 1)

            def copy_v(a, n):
                par = a % 2
                act.wait_ge(v_projected, a * V_GROUPS + n + 1)
                whole = [t for t in group(n) if t < FULL_TILES]
                w = len(whole)
                o = v[:, dyn(par), whole[0]:whole[0] + w, 0:DH].rearrange("p a t c -> p (a t) c")
                last = act.activation(o, X[:, n % 2, 0:w * DH].rearrange("p (t c) -> p t c", c=DH), ACT.Copy)
                if w < len(group(n)):
                    o = v[0:TAIL, dyn(par), FULL_TILES, 0:DH].rearrange("p a c -> p (a c)")
                    last = act.activation(o, X[0:TAIL, n % 2, w * DH:(w + 1) * DH], ACT.Copy)
                last.then_inc(v_high, 1)

            def place_top(m):
                act.wait_ge(top_spread, m + 1)
                o = qd[DH:P, dyn(m % 2), :].rearrange("p a q -> p (a q)")
                act.activation(o, X[DH:P, :, :].rearrange("p a q -> p (a q)"), ACT.Copy, scale=-1.0, bias=LIFT)\
                   .then_inc(top_placed, 1)

            def copy_slot(m, j, half, c, slot, banks=X):
                act.wait_ge(max_scored, m * MAX_SLOTS + slot + 1)
                if c == 0:
                    act.wait_ge(max_reduced, m * TOKEN_TILES + j - 1 + REDUCED0)
                    o = running[half]
                else:
                    act.wait_ge(max_taken, (m * TOKEN_TILES + j) * (MAX_CHUNKS - 1) + c - 2 + TAKEN0)
                    o = scores16[c % 2]
                act.activation(o[:, :], banks[:, :, :].rearrange("p a q -> p (a q)"), ACT.Copy).then_inc(max_copied, 1)

            def exp(b, t, tile, n=P):
                act.wait_ge(scored, b * KEY_TILES + tile + 1)
                if t >= 2:
                    act.wait_ge(applied, b * KEY_TILES + tile - 1)
                act.activation(prob[t % 2][0:n, :], S[t % 2][0:n, :], ACT.Exp, scale=SCALE).then_inc(exp_done, 1)

            def attend(b, with_max):
                m = b + 1
                exp(b, 0, 0)
                for u in range(BODY):
                    exp(b, u + 1, u + 1)
                    if with_max:
                        copy_slot(m, u // MAX_CHUNKS, u // MAX_CHUNKS, u % MAX_CHUNKS, u)
                with act.Fori(1, BODIES) as jj:
                    for u in range(BODY):
                        exp(b, BODY + u + 1, jj * BODY + u + 1)
                        if with_max:
                            copy_slot(m, jj * 2 + u // MAX_CHUNKS, u // MAX_CHUNKS, u % MAX_CHUNKS, jj * BODY + u)
                for t in range(LOOP_TILES + 1, KEY_TILES):
                    exp(b, t, t, TAIL if t == FULL_TILES else P)

            act.wait_ge(constants, 1)
            act.activation(warm[:, :], zeros[0:1, 0:1], ACT.Exp).then_inc(exp_done, 1)
            project(0, FIRST)
            for u in range(BODY):
                copy_slot(0, u // MAX_CHUNKS, u // MAX_CHUNKS, u % MAX_CHUNKS, u, SLOT_BANKS[u % 2])
            with act.Fori(1, BODIES) as jj:
                for u in range(BODY):
                    copy_slot(0, jj * 2 + u // MAX_CHUNKS, u // MAX_CHUNKS, u % MAX_CHUNKS, jj * BODY + u,
                              SLOT_BANKS[u % 2])
            project(1, SECOND)
            attend(0, True)
            with act.Fori(1, HEADS - 1) as h:
                project(h + 1, INNER_HEAD)
                attend(h, True)
            project(HEADS, AFTER_LAST)
            attend(HEADS - 1, False)

        @block.vector
        def _(dve):
            def split_k(a, c):
                par = a % 2
                dve.wait_ge(k_high, a * K_CHUNKS + c + 1)
                k = slice(c * BANK, c * BANK + kwidth(c))
                o = kd[0:DH, dyn(par), k].rearrange("p a q -> p (a q)")
                h = kc[0:DH, dyn(par), k].rearrange("p a q -> p (a q)")
                dve.tensor_tensor(o, bank(c)[0:DH, :], h, op=ALU.subtract).then_inc(k_split, 1)

            def split_v(a, g):
                par = a % 2
                dve.wait_ge(v_high, a * V_GROUPS + g + 1)
                whole = [t for t in group(g) if t < FULL_TILES]
                n = len(whole)
                tt = slice(whole[0], whole[0] + n)
                o = v[:, dyn(par), tt, DH + 1:VCOLS].rearrange("p a t c -> p (a t) c")
                h = v[:, dyn(par), tt, 0:DH].rearrange("p a t c -> p (a t) c")
                x = X[:, g % 2, 0:n * DH].rearrange("p (t c) -> p t c", c=DH)
                last = dve.tensor_tensor(o, x, h, op=ALU.subtract)
                if n < len(group(g)):
                    o = v[0:TAIL, dyn(par), FULL_TILES, DH + 1:VCOLS].rearrange("p a c -> p (a c)")
                    h = v[0:TAIL, dyn(par), FULL_TILES, 0:DH].rearrange("p a c -> p (a c)")
                    last = dve.tensor_tensor(o, X[0:TAIL, g % 2, n * DH:(n + 1) * DH], h, op=ALU.subtract)
                last.then_inc(v_split, 1)

            def split_q(a, i):
                par = a % 2
                dve.wait_ge(q_high, a * 2 + i + 1)
                k = slice(i * BANK, (i + 1) * BANK)
                top_half = qc[0:DH, dyn(par), k].rearrange("p a q -> p (a q)")
                low_half = qc[DH:P, dyn(par), k].rearrange("p a q -> p (a q)")
                dve.tensor_copy(qd[0:DH, dyn(par), k].rearrange("p a q -> p (a q)"), top_half).then_inc(q_split, 1)
                dve.tensor_tensor(low_half, X[DH:P, i, :], low_half, op=ALU.subtract).then_inc(q_split, 1)

            def project(a, kind):
                for what, n in between_heads(kind):
                    if what == "k":
                        split_k(a, n)
                    elif what == "rest":
                        rest_step(a - 1, n)
                    elif what == "fold":
                        fold_tile(a - 1, TOKEN_TILES - 1, 1)
                    elif what == "finish":
                        finish_max(a - 1)
                    elif what == "tail_split":
                        split(a - 2, FULL_TILES, FULL_TILES, TAIL)
                    elif what == "norm":
                        normalize_head(a - 2)
                    elif what == "q":
                        split_q(a, n)
                    elif what == "v":
                        split_v(a, n)

            def take_slot(m, j, half, c, slot, fold=True):
                dve.wait_ge(max_copied, m * MAX_SLOTS + slot + 1)
                r = running[half]
                if c:
                    taken = (m * TOKEN_TILES + j) * (MAX_CHUNKS - 1) + c + TAKEN0
                    if c > 1:
                        dve.wait_ge(max_taken, taken - 1)
                    dve.tensor_tensor(r[:, :], r[:, :], scores16[c % 2][:, :], op=ALU.max).then_inc(max_taken, 1)
                if c == MAX_CHUNKS - 1 and fold:
                    fold_tile(m, j, half)

            def fold_tile(m, j, half):
                r = running[half]
                dve.wait_ge(max_taken, (m * TOKEN_TILES + j + 1) * (MAX_CHUNKS - 1) + TAKEN0)
                dve.tensor_tensor(r[:, 0:BANK], r[:, 0:BANK], r[:, BANK:2 * BANK], op=ALU.max).then_inc(folded, 1)
                dve.wait_ge(folded, m * TOKEN_TILES + j + 1)
                dve.tensor_reduce(loop_max[:, dyn(j)], r[:, 0:BANK], axis=AX.X, op=ALU.max).then_inc(max_reduced, 1)

            def rest_step(m, r):
                dve.wait_ge(rest_scored, m * REST_STEPS + r + 1)
                dve.tensor_reduce(rest_max[:, 2 * r:2 * r + 2], X[:, :, 0:REST], axis=AX.X, op=ALU.max)\
                   .then_inc(rest_reduced, 1)

            def finish_max(m):
                dve.wait_ge(rest_reduced, (m + 1) * REST_STEPS)
                dve.wait_ge(max_reduced, (m + 1) * TOKEN_TILES + REDUCED0)
                dve.tensor_tensor(top[:, :], loop_max[:, :], rest_max[:, :], op=ALU.max).then_inc(top_ready, 1)

            def split(b, t, tile, n=P):
                dve.wait_ge(exp_done, EXP0 + b * KEY_TILES + tile + 1)
                p = prob[t % 2][0:n, :]
                dve.tensor_tensor(prob_low[t % 2][0:n, :], p, p.bitcast(BF16)[:, 1:2 * TOKENS:2], op=ALU.subtract)\
                   .then_inc(prob_split, 1)

            def take_before(m, jj, u, first=False):
                if u:
                    j, c = jj * 2 + (u - 1) // MAX_CHUNKS, (u - 1) % MAX_CHUNKS
                    take_slot(m, j, (u - 1) // MAX_CHUNKS, c, jj * BODY + u - 1, fold=False)
                    if c == 0 and not (first and u == 1):
                        fold_tile(m, j - 1, 1 - (u - 1) // MAX_CHUNKS)
                elif not first:
                    take_slot(m, jj * 2 - 1, 1, MAX_CHUNKS - 1, jj * BODY - 1, fold=False)

            def attend(b, with_max):
                m = b + 1
                for u in range(BODY):
                    split(b, u, u)
                    if with_max:
                        take_before(m, 0, u, first=True)
                with dve.Fori(1, BODIES) as jj:
                    for u in range(BODY):
                        split(b, u, jj * BODY + u)
                        if with_max:
                            take_before(m, jj, u)
                for t in range(LOOP_TILES, FULL_TILES if with_max else KEY_TILES):
                    split(b, t, t, TAIL if t == FULL_TILES else P)
                    if with_max:
                        if t == LOOP_TILES:
                            take_before(m, BODIES, 0)
                        rest_step(m, t - LOOP_TILES)

            def normalize_head(b):
                dve.wait_ge(applied, (b + 1) * KEY_TILES)
                sums = O[:, :, 0:4 * (DH + 1)].rearrange("p b (j c) -> p b j c", c=DH + 1)
                r = rden[:, :].rearrange("p (b j) -> p b j", b=2)
                dve.reciprocal(r, sums[:, :, :, DH]).then_inc(inverted, 1)
                dve.wait_ge(inverted, b + 1)
                for i in range(2):
                    o = att[:, 4 * i:4 * i + 4, dyn(b * DH, DH)]
                    last = dve.tensor_tensor(o, sums[:, i, :, 0:DH], spread_columns(rden[:, 4 * i:4 * i + 4], DH),
                                             op=ALU.mult)
                last.then_inc(normalized, 1)

            dve.memset(zeros[:, :], 0.0).then_inc(constants, 1)
            dve.memset(kd[0:DH, :, KEYS:KEY_COLS], 0.0).then_inc(constants, 1)
            dve.memset(kc[:, :, KEYS:KEY_COLS], 0.0).then_inc(constants, 1)
            dve.memset(top[:, 0:1], 0.0).then_inc(normalized, NORM0)
            dve.memset(top[:, 1:2], 0.0).then_inc(max_taken, TAKEN0)
            dve.memset(top[:, 2:3], 0.0).then_inc(max_reduced, REDUCED0)
            dve.wait_ge(normalized, 1)
            dve.wait_ge(max_taken, TAKEN0)
            dve.wait_ge(max_reduced, REDUCED0)
            project(0, FIRST)
            for u in range(BODY):
                take_slot(0, u // MAX_CHUNKS, u // MAX_CHUNKS, u % MAX_CHUNKS, u)
            with dve.Fori(1, BODIES) as jj:
                for u in range(BODY):
                    take_slot(0, jj * 2 + u // MAX_CHUNKS, u // MAX_CHUNKS, u % MAX_CHUNKS, jj * BODY + u)
            for r in range(REST_STEPS - 2):
                rest_step(0, r)
            project(1, SECOND)
            attend(0, True)
            with dve.Fori(1, HEADS - 1) as h:
                project(h + 1, INNER_HEAD)
                attend(h, True)
            project(HEADS, AFTER_LAST)
            attend(HEADS - 1, False)
            normalize_head(HEADS - 1)


def stage_attention_out(nc, pers, A):
    sc = Scope(nc, "wout", pers.whole)
    KT = HEADS * DH // P
    with sc:
        wout = sc.sb("w", [P, KT, D])
        att_t = [sc.sb(f"att_t{n}", [P, KT, P]) for n in range(2)]
        T = [pers.banks[:, 2 * n:2 * n + 2, :].rearrange("p b (k q) -> p (b k) q", q=P) for n in range(2)]
        Y = [pers.banks[:, 4 + n, 0:D] for n in range(2)]
        w_in, transposed, front_copied, back_copied, multiplied, added = (
            sc.sem(n) for n in ("w_in", "transposed", "front_copied", "back_copied", "multiplied", "added"))
        X, att, ident = pers.X, pers.att, pers.ident
        block = sc.enter_context(nc.Block())

        @block.sync
        def _(sp):
            sp.dma_start(wout[:, :, :], A["wout"].rearrange("(k p) d -> p k d", p=P)).then_inc(w_in, 16)

        @block.tensor
        def _(pe):
            def transpose(j):
                if j >= 2:
                    pe.wait_ge(front_copied, j - 1)
                    pe.wait_ge(back_copied, j - 1)
                for k in range(KT):
                    last = pe.transpose(T[j % 2][:, k, :], att[:, j, k * P:(k + 1) * P], ident[:, :])
                last.then_inc(transposed, 1)

            transpose(0)
            pe.wait_ge(w_in, 16)
            for j in range(TOKEN_TILES):
                if j + 1 < TOKEN_TILES:
                    transpose(j + 1)
                pe.wait_ge(front_copied, j + 1)
                pe.wait_ge(back_copied, j + 1)
                if j >= 2:
                    pe.wait_ge(added, j - 1)
                for k in range(KT):
                    last = pe.matmul(Y[j % 2][:, :], att_t[j % 2][:, k, :], wout[:, k, :], start=k == 0,
                                     stop=k == KT - 1)
                last.then_inc(multiplied, 1)

        def copy(eng, j, half):
            eng.wait_ge(transposed, j + 1)
            if j >= 2:
                eng.wait_ge(multiplied, j - 1)
            k = slice(half * KT // 2, (half + 1) * KT // 2)
            return att_t[j % 2][:, k, :], T[j % 2][:, k, :]

        @block.scalar
        def _(act):
            for j in range(TOKEN_TILES):
                o, i = copy(act, j, 0)
                act.activation(o, i, ACT.Copy).then_inc(front_copied, 1)

        @block.vector
        def _(dve):
            for j in range(TOKEN_TILES + 1):
                if j < TOKEN_TILES:
                    o, i = copy(dve, j, 1)
                    dve.tensor_copy(o, i).then_inc(back_copied, 1)
                if j >= 1:
                    dve.wait_ge(multiplied, j)
                    dve.tensor_tensor(X[:, j - 1, :], Y[(j - 1) % 2][:, :], X[:, j - 1, :], op=ALU.add)\
                       .then_inc(added, 1)


def stage_experts(nc, pers, A, name, layer, out=None, ahead=None):
    sc = Scope(nc, name, pers.whole)
    second = layer == 1
    W = P // GROUP
    with sc:
        n = sc.sb("n", [P, TOKEN_TILES, D])
        n_t = sc.sb("n_t", [P, TOKENS])
        control = sc.sb("control", [P, ES])
        up = pers.next_up if second else sc.sb("up", [P, ES, ESIZE])
        down = sc.sb("down", [P, EXPERTS, D])
        up_bias = sc.sb("up_bias", [EXPERTS, P])
        up_bias_t = sc.sb("up_bias_t", [P, EXPERTS])
        tie = sc.sb("tie", [P, GROUP])
        logits = sc.sb("logits", [P, GROUPS, GROUP])
        largest = sc.sb("largest", [P, GROUPS])
        pick_t = sc.sb("pick_t", [P, GROUPS, GROUP])
        pick = sc.sb("pick", [P, TOKEN_TILES, W, ES])
        taken_t = sc.sb("taken_t", [P, GROUPS, ES])
        hidden = sc.sb("hidden", [P, EXPERTS, SETS, GROUPS])
        biased = sc.sb("biased", [P, EXPERTS, GROUPS])
        result_t = sc.sb("result_t", [P, ES, GROUPS])
        result = sc.sb("result", [P, GROUPS, D])
        if second:
            control_bias = sc.sb("control_bias", [P, 1])
            down_bias = sc.sb("down_bias", [P, D])
            down_raw = pers.next_down
        ns = NormState(sc, "ns", TOKEN_TILES)
        NB = 8
        B = [pers.banks[:, i, :] for i in range(NB)]
        names = ("control_in up_in down_in bias_in tie_ready vec normalized transposed copied scored picked "
                 "pick_transposed pick_zeroed pick_copied took took_copied up_done hidden_zeroed biased_ready "
                 "hidden_front hidden_back bias_transposed "
                 "bias_copied down_transposed down_copied down_done down_read result_transposed result_copied "
                 "returned added stored").split()
        s = {x: sc.sem(x) for x in names}
        X, ident = pers.X, pers.ident
        block = sc.enter_context(nc.Block())

        @block.sync
        def _(sp):
            sp.dma_start(control[:, :], A["control"].rearrange("d e s -> d (e s)")).then_inc(s["control_in"], 16)
            if second:
                sp.dma_start(control_bias[:, :], A["control_bias"].rearrange("e (s one) -> (e s) one", one=1))\
                  .then_inc(s["control_in"], 16)
            else:
                sp.dma_start(up[:, :, :], A["up"].rearrange("d e s f -> d (e s) f")).then_inc(s["up_in"], 16)
                sp.wait_ge(s["up_in"], 16)
                sp.wait_ge(s["down_in"], 16)
                sp.dma_start(pers.ctx[:, :, :], ahead["ctx"][0, 0:CTX_ROWS, :].rearrange("(p t) d -> p t d", p=P))\
                  .then_inc(pers.ctx_in, 16)
                sp.dma_start(pers.ctx_tail[:, :], ahead["ctx"][0, CTX_ROWS:CONTEXT, :]).then_inc(pers.ctx_in, 16)
                sp.dma_start(pers.next_up[:, :, :], ahead["up"].rearrange("e s d f -> d (e s) f"))\
                  .then_inc(pers.next_in, 16)
                sp.dma_start(pers.next_down[:, :, :].rearrange("p e (s f) -> p (e s) f", f=ESIZE),
                             ahead["down"].rearrange("e s d f -> d (e s) f")).then_inc(pers.next_in, 16)
            if out is not None:
                view = out[0].rearrange("(t p) d -> p t d", p=P)
                for i in range(2):
                    sp.wait_ge(s["added"], i + 1)
                    sp.dma_start(view[:, 4 * i:4 * i + 4, :], X[:, 4 * i:4 * i + 4, :]).then_inc(s["stored"], 16)
                sp.wait_ge(s["stored"], 32)

        @block.gpsimd
        def _(pool):
            for t in range(GROUP):
                last = pool.memset(tie[:, t:t + 1], t * TIE_STEP)
            last.then_inc(s["tie_ready"], 1)
            pool.memset(pick[:, :, :, :], 0.0).then_inc(s["pick_zeroed"], 1)
            pool.memset(hidden[:, :, :, :], 0.0).then_inc(s["hidden_zeroed"], 1)

        @block.scalar
        def _(act):
            act.dma_start(up_bias[:, :], A["up_bias"].rearrange("e s f -> e (s f)")).then_inc(s["bias_in"], 16)
            if second:
                act.dma_start(down_bias[:, :], A["down_bias"].rearrange("e s d -> (e s) d")).then_inc(s["bias_in"], 16)
            else:
                act.dma_start(down[:, :, :], A["down"].rearrange("e s f d -> (s f) e d")).then_inc(s["down_in"], 16)
            norm_sqrt(act, ns, 0, TOKEN_TILES, 1)
            for i in range(2):
                act.wait_ge(s["transposed"], i + 1)
                act.activation(n_t[:, i * BANK:(i + 1) * BANK], B[i][:, :], ACT.Copy).then_inc(s["copied"], 1)
            act.wait_ge(s["bias_transposed"], 1)
            act.activation(up_bias_t[:, :], B[6][:, 0:EXPERTS], ACT.Copy).then_inc(s["bias_copied"], 1)
            if second:
                for k in range(EXPERTS // W):
                    act.wait_ge(s["down_transposed"], k + 1)
                    act.activation(down[:, 4 * k:4 * k + 4, :], B[6 + k % 2][:, :].rearrange("p (e d) -> p e d", d=D),
                                   ACT.Copy).then_inc(s["down_copied"], 1)
            act.wait_ge(s["pick_zeroed"], 1)
            for i in range(2):
                act.wait_ge(s["pick_transposed"], i + 1)
                for g in range(W):
                    r = slice(g * GROUP, (g + 1) * GROUP)
                    last = act.activation(pick[r, 4 * i:4 * i + 4, g, :],
                                          B[i][r, :].rearrange("p (t c) -> p t c", c=ES), ACT.Copy)
                last.then_inc(s["pick_copied"], 1)
            act.wait_ge(s["biased_ready"], 2)
            act.wait_ge(s["hidden_zeroed"], 1)
            for q in (0, 1):
                r = slice(q * ESIZE, (q + 1) * ESIZE)
                last = act.activation(hidden[r, :, q, :], biased[r, :, :], ACT.Relu)
            last.then_inc(s["hidden_front"], 1)
            for k in range(EXPERTS // W):
                act.wait_ge(s["down_done"], k + 1)
                act.activation(result_t[:, k * 4 * SETS:(k + 1) * 4 * SETS, :],
                               B[k % 4][:, :].rearrange("p (c g) -> p c g", g=GROUPS), ACT.Copy)\
                   .then_inc(s["down_read"], 1)

        @block.vector
        def _(dve):
            steps = Steps(dve, s["vec"])
            for t in range(TOKEN_TILES):
                last = dve.bn_stats(ns.stats[:, t, :], X[:, t, :])
            steps.link(last)
            norm_moments(dve, steps, ns, 0, TOKEN_TILES)
            norm_rstd(dve, steps, ns, 0, TOKEN_TILES, 1)
            for t in range(TOKEN_TILES):
                normalize(dve, n[:, t, :], X[:, t, :], ns, t).then_inc(s["normalized"], 1)
            dve.wait_ge(s["tie_ready"], 1)
            if second:
                dve.wait_ge(s["control_in"], 32)
            H = GROUPS // 2
            tied = tie[:, :].rearrange("p (one t) -> p one t", one=1).to_broadcast([P, H, GROUP])
            for i in range(2):
                dve.wait_ge(s["scored"], i + 1)
                g = slice(i * H, (i + 1) * H)
                bias = control_bias[:, 0:1] if second else 0.0
                steps.link(dve.scalar_tensor_tensor(logits[:, g, :], B[2 + i][:, :].rearrange("p (g t) -> p g t", t=GROUP),
                                                    bias, tied, ALU.add, ALU.add))
                steps.link(dve.tensor_reduce(largest[:, g], logits[:, g, :], axis=AX.X, op=ALU.max))
                dve.tensor_tensor(pick_t[:, g, :], logits[:, g, :], spread_columns(largest[:, g], GROUP),
                                  op=ALU.is_equal).then_inc(s["picked"], 1)
            for t in range(TOKEN_TILES):
                dve.wait_ge(s["took"], t + 1)
                dve.tensor_copy(taken_t[:, W * t:W * (t + 1), :], B[2 + t % 4][:, :].rearrange("p (g c) -> p g c", c=ES))\
                   .then_inc(s["took_copied"], 1)
            dve.wait_ge(s["bias_copied"], 1)
            for i in range(2):
                dve.wait_ge(s["up_done"], i + 1)
                e = slice(i * EXPERTS // 2, (i + 1) * EXPERTS // 2)
                dve.tensor_tensor(biased[:, e, :], B[i][:, :].rearrange("p (e g) -> p e g", g=GROUPS),
                                  spread_columns(up_bias_t[:, e], GROUPS), op=ALU.add).then_inc(s["biased_ready"], 1)
            dve.wait_ge(s["biased_ready"], 2)
            dve.wait_ge(s["hidden_zeroed"], 1)
            for q in (2, 3):
                r = slice(q * ESIZE, (q + 1) * ESIZE)
                last = dve.tensor_scalar(hidden[r, :, q, :], biased[r, :, :], 0.0, None, ALU.max)
            last.then_inc(s["hidden_back"], 1)
            for k in range(GROUPS // 4):
                dve.wait_ge(s["result_transposed"], k + 1)
                o = result[:, 4 * k:4 * k + 4, :]
                i_ = B[4 + k % 2][:, :].rearrange("p (g d) -> p g d", d=D)
                if second:
                    if k == 0:
                        dve.wait_ge(s["bias_in"], 32)
                    b = down_bias[:, :].rearrange("p (one d) -> p one d", one=1).to_broadcast([P, 4, D])
                    dve.tensor_tensor(o, i_, b, op=ALU.add).then_inc(s["result_copied"], 1)
                else:
                    dve.tensor_copy(o, i_).then_inc(s["result_copied"], 1)
            for i in range(2):
                dve.wait_ge(s["returned"], i + 1)
                x = X[:, 4 * i:4 * i + 4, :]
                dve.tensor_tensor(x, B[6 + i][:, :].rearrange("p (t d) -> p t d", d=D), x, op=ALU.add)\
                   .then_inc(s["added"], 1)

        @block.tensor
        def _(pe):
            for t in range(TOKEN_TILES):
                pe.wait_ge(s["normalized"], t + 1)
                last = pe.transpose(B[t // 4][:, (t % 4) * P:(t % 4 + 1) * P], n[:, t, :], ident[:, :])
                if t % 4 == 3:
                    last.then_inc(s["transposed"], 1)
            pe.wait_ge(s["control_in"], 32 if second else 16)
            for i in range(2):
                pe.wait_ge(s["copied"], i + 1)
                pe.matmul(B[2 + i][:, :], control[:, :], n_t[:, i * BANK:(i + 1) * BANK], start=True, stop=True)\
                  .then_inc(s["scored"], 1)
            pe.wait_ge(s["bias_in"], 32 if second else 16)
            pe.transpose(B[6][:, 0:EXPERTS], up_bias[:, :], ident[0:EXPERTS, 0:EXPERTS]).then_inc(s["bias_transposed"], 1)
            if second:
                pe.wait_ge(pers.next_in, 32)
                for k in range(EXPERTS // W):
                    pe.wait_ge(s["bias_copied"], 1)
                    if k >= 2:
                        pe.wait_ge(s["down_copied"], k - 1)
                    for e in range(4):
                        last = pe.transpose(B[6 + k % 2][:, e * P:(e + 1) * P], down_raw[:, 4 * k + e, :], ident[:, :])
                    last.then_inc(s["down_transposed"], 1)
            for i in range(2):
                pe.wait_ge(s["picked"], i + 1)
                for t in range(4 * i, 4 * i + 4):
                    last = pe.transpose(B[i][:, (t % 4) * P:(t % 4 + 1) * P],
                                        pick_t[:, :, :].rearrange("p g t -> p (g t)")[:, t * P:(t + 1) * P], ident[:, :])
                last.then_inc(s["pick_transposed"], 1)
            for t in range(TOKEN_TILES):
                if t % 4 == 0:
                    pe.wait_ge(s["pick_copied"], t // 4 + 1)
                if t >= 4:
                    pe.wait_ge(s["took_copied"], t - 3)
                pe.matmul(B[2 + t % 4][:, :], n[:, t, :], pick[:, t, :, :].rearrange("p g c -> p (g c)"),
                          start=True, stop=True).then_inc(s["took"], 1)
            if not second:
                pe.wait_ge(s["up_in"], 16)
            pe.wait_ge(s["took_copied"], TOKEN_TILES)
            for c in range(ES):
                e, q = c // SETS, c % SETS
                o = B[e // 16][q * ESIZE:(q + 1) * ESIZE, (e % 16) * GROUPS:(e % 16 + 1) * GROUPS]
                last = pe.matmul(o, up[:, c, :], taken_t[:, :, c], start=True, stop=True)
                if c % (ES // 2) == ES // 2 - 1:
                    last.then_inc(s["up_done"], 1)
            pe.wait_ge(s["hidden_front"], 1)
            pe.wait_ge(s["hidden_back"], 1)
            if second:
                pe.wait_ge(s["down_copied"], EXPERTS // W)
            else:
                pe.wait_ge(s["down_in"], 16)
            for k in range(EXPERTS // W):
                if k >= 4:
                    pe.wait_ge(s["down_read"], k - 3)
                for e in range(4):
                    last = pe.matmul(B[k % 4][:, e * P:(e + 1) * P], down[:, 4 * k + e, :],
                                     hidden[:, 4 * k + e, :, :].rearrange("p s g -> p (s g)"), start=True, stop=True)
                last.then_inc(s["down_done"], 1)
            pe.wait_ge(s["down_read"], EXPERTS // W)
            for k in range(GROUPS // 4 + 1):
                if k < GROUPS // 4:
                    if k >= 2:
                        pe.wait_ge(s["result_copied"], k - 1)
                    for i in range(4):
                        last = pe.transpose(B[4 + k % 2][:, i * P:(i + 1) * P], result_t[:, :, 4 * k + i], ident[:, :])
                    last.then_inc(s["result_transposed"], 1)
                if k >= 1:
                    j = k - 1
                    pe.wait_ge(s["result_copied"], k)
                    for i in range(W):
                        g = 4 * j + i
                        last = pe.matmul(B[6 + j // 4][i * GROUP:(i + 1) * GROUP, (j % 4) * D:(j % 4 + 1) * D],
                                         pick_t[:, g, :], result[:, g, :], start=True, stop=True)
                    if j % 4 == 3:
                        last.then_inc(s["returned"], 1)


def stage_cross(nc, pers, A):
    sc = Scope(nc, "cross", pers.whole)
    QT = CTX_TILES + 1
    QC = -(-CONTEXT // BANK)
    PIECES = -(-QC // 2)
    AHEAD = 3
    SCORED_BY = QC - 1 - AHEAD
    APPLY_LAG = 2
    with sc:
        ctx, tail = pers.ctx, pers.ctx_tail
        ctx_h = sc.sb("ctx_h", [P, QT, D], F16)
        ctx_l = sc.sb("ctx_l", [P, QT, D], F16)
        q_h = sc.sb("q_h", [P, CONTEXT], F16)
        q_l = sc.sb("q_l", [P, CONTEXT], F16)
        c = sc.sb("c", [P, TOKEN_TILES, D])
        c_t = sc.sb("c_t", [P, TOKENS])
        m_t = sc.sb("m_t", [P, TOKENS])
        m_h = sc.sb("m_h", [P, TOKENS], F16)
        m_l = sc.sb("m_l", [P, TOKENS], F16)
        w = sc.sb("w", [P, 3])
        bs = sc.sb("bs", [P, 4])
        scores = sc.sb("scores", [P, 2, CONTEXT])
        NPT = 3
        pt_h = sc.sb("pt_h", [P, NPT, BANK], F16)
        pt_l = sc.sb("pt_l", [P, NPT, BANK], F16)
        chunk_max = sc.sb("chunk_max", [P, QC])
        top = sc.sb("top", [P, TOKEN_TILES])
        neg_top = sc.sb("neg_top", [P, TOKEN_TILES])
        den_parts = sc.sb("den_parts", [P, TOKEN_TILES, PIECES])
        den = sc.sb("den", [P, TOKEN_TILES])
        rden = sc.sb("rden", [P, TOKEN_TILES])
        c2q = sc.sb("c2q", [P, TOKEN_TILES, D])
        c2q_t = sc.sb("c2q_t", [P, TOKENS])
        mixed_t = m_t
        back_t = sc.sb("back_t", [P, TOKENS])
        wl = sc.sb("wl", [P, 4, P])
        wl_t = sc.sb("wl_t", [P, 4, P])
        bl = sc.sb("bl", [P, D])
        level = sc.sb("level", [P, TOKEN_TILES])
        level_max = sc.sb("level_max", [P, 1])
        all_max = sc.sb("all_max", [P, 1])
        neg_all_max = sc.sb("neg_all_max", [P, 1])
        row_max = sc.sb("row_max", [1, P])
        one_max = sc.sb("one_max", [1, 1])
        b_att = sc.sb("b_att", [P, TOKEN_TILES])
        ones = sc.sb("ones", [P, P])
        q2c = sc.sb("q2c", [P, 1])
        rsum = sc.sb("rsum", [P, 1])
        ns = NormState(sc, "ns", TOKEN_TILES)
        B = [pers.banks[:, i, :] for i in range(8)]
        names = ("w_in bl_in vec normalized transposed copied m_ready m_high m_split q_transposed "
                 "q_high q_split rows_high rows_split tail_split scored stored max_ready exponents probs_t "
                 "probs_high probs_split "
                 "applied applied_read ready_ones wl_transposed wl_copied level_done level_ready row_ready "
                 "one_ready spread spread_read weights_ready summed c2q_transposed "
                 "c2q_copied factors projected added").split()
        s = {x: sc.sem(x) for x in names}
        X, ident = pers.X, pers.ident
        block = sc.enter_context(nc.Block())

        def width(k):
            return min(BANK, CONTEXT - k * BANK)

        def tiles_of(k):
            return list(range(4 * k, min(4 * k + 4, QT)))

        def rows(t):
            return TAIL if t == CTX_TILES else P

        def spans(k):
            whole = len([t for t in tiles_of(k) if t < CTX_TILES])
            out = [(0, whole * P, P)] if whole else []
            if CTX_TILES in tiles_of(k):
                out.append((whole * P, (whole + 1) * P, TAIL))
            return out

        def scored_in(k):
            if k < AHEAD:
                return [2 * k, 2 * k + 1]
            return [k + AHEAD] if k <= SCORED_BY else []

        @block.gpsimd
        def _(pool):
            pool.memset(ones[:, :], 1.0).then_inc(s["ready_ones"], 1)
            pool.wait_ge(s["ready_ones"], 1)
            for k in range(QC):
                pool.wait_ge(s["rows_high"], k + 2)
                t = slice(4 * k, min(4 * k + 4, CTX_TILES))
                if k:
                    pool.wait_ge(s["rows_split"], k)
                pool.tensor_tensor(ctx_l[:, t, :], ctx[:, t, :], ctx_h[:, t, :], op=ALU.subtract)\
                    .then_inc(s["rows_split"], 1)

        @block.scalar
        def _(act):
            for i, v in enumerate((A["w_cq"], A["w_q"], A["w_c"])):
                act.dma_start(w[:, i:i + 1], column(v)).then_inc(s["w_in"], 16)
            for i, v in enumerate((A["b_c"], A["b_q"], A["b_cq"])):
                act.dma_start(bs[:, i:i + 1], v.partition_broadcast(P)).then_inc(s["w_in"], 16)
            act.dma_start(wl[:, :, :], A["w_l"].rearrange("o (k i) -> o k i", k=4)).then_inc(s["w_in"], 16)
            act.dma_start(bl[:, :], A["b_l"].partition_broadcast(P)).then_inc(s["bl_in"], 16)
            norm_sqrt(act, ns, 0, TOKEN_TILES, 1)
            for i in range(2):
                act.wait_ge(s["transposed"], i + 1)
                act.activation(c_t[:, i * BANK:(i + 1) * BANK], B[i][:, :], ACT.Copy).then_inc(s["copied"], 1)
            act.wait_ge(s["m_ready"], 1)
            act.activation(m_h[:, :], m_t[:, :], ACT.Copy).then_inc(s["m_high"], 1)
            act.wait_ge(pers.ctx_in, 32)
            act.activation(ctx_h[0:TAIL, CTX_TILES, :], tail[:, :], ACT.Copy).then_inc(s["rows_high"], 1)
            for k in range(QC):
                act.wait_ge(s["q_transposed"], k + 1)
                act.activation(q_h[:, k * BANK:k * BANK + width(k)], B[3 + k % 3][:, 0:width(k)], ACT.Copy)\
                   .then_inc(s["q_high"], 1)
                t = slice(4 * k, min(4 * k + 4, CTX_TILES))
                act.activation(ctx_h[:, t, :], ctx[:, t, :], ACT.Copy).then_inc(s["rows_high"], 1)
            act.wait_ge(s["wl_transposed"], 1)
            act.activation(wl_t[:, :, :].rearrange("p k o -> p (k o)"), B[6][:, :], ACT.Copy).then_inc(s["wl_copied"], 1)

            def exponents(i, p):
                act.wait_ge(s["max_ready"], i + 1)
                x = scores[:, i % 2, 2 * p * BANK:min(2 * (p + 1) * BANK, CONTEXT)]
                act.activation(x, x, ACT.Exp, bias=neg_top[:, i:i + 1], accum_out=den_parts[:, i, p:p + 1])\
                   .then_inc(s["exponents"], 1)

            exponents(0, 0)
            for i in range(TOKEN_TILES):
                for k in range(QC):
                    if k % 2 == 0 and k // 2 + 1 < PIECES:
                        exponents(i, k // 2 + 1)
                    if k == QC - 1 and i + 1 < TOKEN_TILES:
                        exponents(i + 1, 0)
                    act.wait_ge(s["probs_t"], i * QC + k + 1)
                    if i * QC + k >= NPT:
                        act.wait_ge(s["applied"], i * QC + k - NPT + 1)
                    x = (i * QC + k) % NPT
                    for lo, hi, n in spans(k):
                        last = act.activation(pt_h[0:n, x, lo:hi], B[3 + (i * QC + k) % 3][0:n, lo:hi], ACT.Copy)
                    last.then_inc(s["probs_high"], 1)
            act.wait_ge(s["spread_read"], 1)
            act.activation(b_att[:, :], level[:, :], ACT.Exp, bias=neg_all_max[:, 0:1]).then_inc(s["weights_ready"], 1)
            for i in range(2):
                act.wait_ge(s["c2q_transposed"], i + 1)
                act.activation(c2q_t[:, i * BANK:(i + 1) * BANK], B[i][:, :], ACT.Copy).then_inc(s["c2q_copied"], 1)

        @block.vector
        def _(dve):
            steps = Steps(dve, s["vec"])
            for t in range(TOKEN_TILES):
                last = dve.bn_stats(ns.stats[:, t, :], X[:, t, :])
            steps.link(last)
            norm_moments(dve, steps, ns, 0, TOKEN_TILES)
            norm_rstd(dve, steps, ns, 0, TOKEN_TILES, 1)
            for t in range(TOKEN_TILES):
                normalize(dve, c[:, t, :], X[:, t, :], ns, t).then_inc(s["normalized"], 1)
            dve.wait_ge(s["w_in"], 16 * 7)
            steps.done(dve.tensor_tensor(bs[:, 3:4], bs[:, 0:1], bs[:, 1:2], op=ALU.add))
            dve.wait_ge(steps.sem, steps.count)
            steps.link(dve.tensor_tensor(bs[:, 3:4], bs[:, 3:4], bs[:, 2:3], op=ALU.add))
            dve.wait_ge(s["copied"], 2)
            dve.tensor_scalar(m_t[:, :], c_t[:, :], w[:, 0:1], w[:, 1:2], ALU.mult, ALU.add).then_inc(s["m_ready"], 1)
            dve.wait_ge(s["m_high"], 1)
            dve.tensor_tensor(m_l[:, :], m_t[:, :], m_h[:, :], op=ALU.subtract).then_inc(s["m_split"], 1)
            dve.wait_ge(s["rows_high"], 1)
            dve.tensor_tensor(ctx_l[0:TAIL, CTX_TILES, :], tail[:, :], ctx_h[0:TAIL, CTX_TILES, :], op=ALU.subtract)\
               .then_inc(s["tail_split"], 1)
            dve.wait_ge(s["level_done"], 1)
            steps.link(dve.tensor_scalar(level[:, :], B[7][:, 0:TOKEN_TILES], bs[:, 3:4], None, ALU.add))

            def store_chunk(i, k):
                x = i * QC + k
                dve.wait_ge(s["scored"], x + 1)
                if k == 0 and i >= 2:
                    dve.wait_ge(s["probs_t"], (i - 1) * QC)
                dve.tensor_scalar(scores[:, i % 2, k * BANK:k * BANK + width(k)], B[x % 3][:, 0:width(k)], 0.0, None,
                                  ALU.add, ALU.max, accum_out=chunk_max[:, k:k + 1]).then_inc(s["stored"], 1)

            def tile_max(i):
                dve.wait_ge(s["stored"], (i + 1) * QC)
                steps.link(dve.tensor_reduce(top[:, i:i + 1], chunk_max[:, :], axis=AX.X, op=ALU.max))
                dve.tensor_scalar(neg_top[:, i:i + 1], top[:, i:i + 1], -1.0, None, ALU.mult).then_inc(s["max_ready"], 1)

            def split_chunk(i, k):
                x = i * QC + k
                dve.wait_ge(s["probs_high"], x + 1)
                for lo, hi, n in spans(k):
                    last = dve.tensor_tensor(pt_l[0:n, x % NPT, lo:hi], B[3 + x % 3][0:n, lo:hi],
                                             pt_h[0:n, x % NPT, lo:hi], op=ALU.subtract)
                last.then_inc(s["probs_split"], 1)

            def finish_tile(i):
                dve.wait_ge(s["applied"], (i + 1) * QC)
                steps.link(dve.tensor_reduce(den[:, i:i + 1], den_parts[:, i, :], axis=AX.X, op=ALU.add))
                steps.link(dve.reciprocal(rden[:, i:i + 1], den[:, i:i + 1]))
                dve.tensor_scalar(c2q[:, i, :], B[6 + i % 2][:, 0:D], rden[:, i:i + 1], None, ALU.mult)\
                   .then_inc(s["applied_read"], 1)

            for k in range(QC):
                dve.wait_ge(s["q_high"], k + 1)
                r = slice(k * BANK, k * BANK + width(k))
                dve.tensor_tensor(q_l[:, r], B[3 + k % 3][:, 0:width(k)], q_h[:, r], op=ALU.subtract)\
                   .then_inc(s["q_split"], 1)
                if k:
                    store_chunk(0, k - 1)
            store_chunk(0, QC - 1)
            tile_max(0)
            for i in range(TOKEN_TILES):
                for k in range(QC):
                    if i + 1 < TOKEN_TILES:
                        for n in scored_in(k):
                            store_chunk(i + 1, n)
                        if k == SCORED_BY:
                            tile_max(i + 1)
                    split_chunk(i, k)
                    if k == APPLY_LAG and i:
                        finish_tile(i - 1)
            finish_tile(TOKEN_TILES - 1)
            steps.link(dve.tensor_tensor(level[:, :], level[:, :], top[:, :], op=ALU.add))
            dve.tensor_reduce(level_max[:, :], level[:, :], axis=AX.X, op=ALU.max).then_inc(s["level_ready"], 1)
            dve.wait_ge(s["row_ready"], 1)
            dve.tensor_reduce(one_max[:, :], B[4][0:1, 0:P], axis=AX.X, op=ALU.max).then_inc(s["one_ready"], 1)
            dve.wait_ge(s["spread"], 1)
            dve.tensor_scalar(neg_all_max[:, :], B[5][:, 0:1], -1.0, None, ALU.mult).then_inc(s["spread_read"], 1)
            dve.wait_ge(s["summed"], 1)
            steps.link(dve.reciprocal(rsum[:, :], B[4][:, 0:1]))
            steps.link(dve.tensor_scalar(q2c[:, :], B[5][:, 0:1], rsum[:, 0:1], None, ALU.mult))
            steps.done(dve.tensor_scalar(back_t[:, :], c_t[:, :], q2c[:, 0:1], None, ALU.mult))
            dve.wait_ge(s["c2q_copied"], 2)
            dve.tensor_tensor(mixed_t[:, :], c_t[:, :], c2q_t[:, :], op=ALU.mult).then_inc(s["factors"], 1)
            dve.wait_ge(s["bl_in"], 16)
            for i in range(2):
                for t in range(4 * i, 4 * i + 4):
                    last = dve.tensor_tensor(X[:, t, :], X[:, t, :], bl[:, :], op=ALU.add)
            steps.link(last)
            for i in range(2):
                dve.wait_ge(s["projected"], i + 1)
                x = X[:, 4 * i:4 * i + 4, :]
                dve.tensor_tensor(x, B[2 + i][:, :].rearrange("p (t d) -> p t d", d=D), x, op=ALU.add)\
                   .then_inc(s["added"], 1)

        @block.tensor
        def _(pe):
            for t in range(TOKEN_TILES):
                pe.wait_ge(s["normalized"], t + 1)
                last = pe.transpose(B[t // 4][:, (t % 4) * P:(t % 4 + 1) * P], c[:, t, :], ident[:, :])
                if t % 4 == 3:
                    last.then_inc(s["transposed"], 1)
            pe.wait_ge(s["w_in"], 16 * 7)
            for k in range(4):
                last = pe.transpose(B[6][:, k * P:(k + 1) * P], wl[:, k, :], ident[:, :])
            last.then_inc(s["wl_transposed"], 1)
            pe.wait_ge(s["copied"], 2)
            for t in range(TOKEN_TILES):
                last = pe.matmul(B[7][:, t:t + 1], c_t[:, t * P:(t + 1) * P], w[:, 2:3], start=True, stop=True)
            last.then_inc(s["level_done"], 1)
            def score(i, k):
                x = i * QC + k
                if x >= 3:
                    pe.wait_ge(s["stored"], x - 2)
                if i == 0:
                    pe.wait_ge(s["q_split"], k + 1)
                ch, cl = (m[:, i * P:(i + 1) * P] for m in (m_h, m_l))
                r = slice(k * BANK, k * BANK + width(k))
                o = B[x % 3][:, 0:width(k)]
                pe.matmul(o, ch, q_h[:, r], start=True, stop=False)
                pe.matmul(o, ch, q_l[:, r], start=False, stop=False)
                pe.matmul(o, cl, q_h[:, r], start=False, stop=True).then_inc(s["scored"], 1)

            def transpose(i, k):
                x = i * QC + k
                if k % 2 == 0:
                    pe.wait_ge(s["exponents"], i * PIECES + k // 2 + 1)
                if x >= 3:
                    pe.wait_ge(s["probs_split"], x - 2)
                for t in tiles_of(k):
                    n = rows(t)
                    last = pe.transpose(B[3 + x % 3][0:n, (t % 4) * P:(t % 4 + 1) * P],
                                        scores[:, i % 2, t * P:t * P + n], ident[:, :])
                last.then_inc(s["probs_t"], 1)

            def apply(i, k):
                x = i * QC + k
                if k == 0 and i >= 2:
                    pe.wait_ge(s["applied_read"], i - 1)
                pe.wait_ge(s["probs_split"], x + 1)
                if i == 0:
                    pe.wait_ge(s["rows_split"], k + 1)
                for t in tiles_of(k):
                    n = rows(t)
                    col = slice((t % 4) * P, (t % 4 + 1) * P)
                    ph, pl = pt_h[0:n, x % NPT, col], pt_l[0:n, x % NPT, col]
                    o = B[6 + i % 2][:, 0:D]
                    pe.matmul(o, ph, ctx_h[0:n, t, :], start=t == 0, stop=False)
                    pe.matmul(o, ph, ctx_l[0:n, t, :], start=False, stop=False)
                    last = pe.matmul(o, pl, ctx_h[0:n, t, :], start=False, stop=t == CTX_TILES)
                last.then_inc(s["applied"], 1)

            pe.wait_ge(pers.ctx_in, 32)
            for k in range(QC):
                if k >= 3:
                    pe.wait_ge(s["q_split"], k - 2)
                for t in tiles_of(k):
                    n = rows(t)
                    src = ctx[:, t, :] if t < CTX_TILES else tail[:, :]
                    last = pe.transpose(B[3 + k % 3][:, (t % 4) * P:(t % 4) * P + n], src, ident[0:n, 0:n])
                last.then_inc(s["q_transposed"], 1)
                if k == 0:
                    pe.wait_ge(s["m_split"], 1)
                else:
                    score(0, k - 1)
            score(0, QC - 1)
            pe.wait_ge(s["wl_copied"], 1)
            pe.wait_ge(s["tail_split"], 1)
            for x in range(TOKEN_TILES * QC + APPLY_LAG):
                i, k = divmod(x, QC)
                if i + 1 < TOKEN_TILES:
                    for n in scored_in(k):
                        score(i + 1, n)
                if i < TOKEN_TILES:
                    transpose(i, k)
                if x >= APPLY_LAG:
                    apply(*divmod(x - APPLY_LAG, QC))
            pe.wait_ge(s["level_ready"], 1)
            pe.wait_ge(s["ready_ones"], 1)
            pe.transpose(B[4][0:1, 0:P], level_max[:, :], ident[:, :]).then_inc(s["row_ready"], 1)
            pe.wait_ge(s["one_ready"], 1)
            pe.matmul(B[5][:, 0:1], ones[0:1, :], one_max[:, :], start=True, stop=True).then_inc(s["spread"], 1)
            pe.wait_ge(s["applied_read"], TOKEN_TILES)
            for t in range(TOKEN_TILES):
                last = pe.transpose(B[t // 4][:, (t % 4) * P:(t % 4 + 1) * P], c2q[:, t, :], ident[:, :])
                if t % 4 == 3:
                    last.then_inc(s["c2q_transposed"], 1)
            pe.wait_ge(s["weights_ready"], 1)
            for t in range(TOKEN_TILES):
                pe.matmul(B[4][:, 0:1], ones[:, :], b_att[:, t:t + 1], start=t == 0, stop=t == TOKEN_TILES - 1)
            for t in range(TOKEN_TILES):
                last = pe.matmul(B[5][:, 0:1], c[:, t, :], b_att[:, t:t + 1], start=t == 0, stop=t == TOKEN_TILES - 1)
            last.then_inc(s["summed"], 1)
            pe.wait_ge(s["factors"], 1)
            for t in range(TOKEN_TILES):
                for n, part in enumerate((c_t, c2q_t, mixed_t, back_t)):
                    last = pe.matmul(B[2 + t // 4][:, (t % 4) * D:(t % 4 + 1) * D], part[:, t * P:(t + 1) * P],
                                     wl_t[:, n, :], start=n == 0, stop=n == 3)
                if t % 4 == 3:
                    last.then_inc(s["projected"], 1)


class Persistent:

    def __init__(self, sc):
        self.whole = sc
        self.X = sc.sb("X", [P, TOKEN_TILES, D])
        self.ident = sc.sb("ident", [P, P])
        self.banks = sc.ps("banks", [P, 8, BANK])


def for_later_stages(pers, sc):
    pers.ctx = sc.sb("ctx", [P, CTX_TILES, D])
    pers.ctx_tail = sc.sb("ctx_tail", [TAIL, D])
    pers.next_up = sc.sb("next_up", [P, ES, ESIZE])
    pers.next_down = sc.sb("next_down", [P, EXPERTS, SETS * ESIZE])
    pers.ctx_in, pers.next_in = sc.sem("ctx_in"), sc.sem("next_in")


def for_attention(pers, sc):
    pers.kvh = sc.sb("kvh", [P, KEYS], F16)
    pers.kvl = sc.sb("kvl", [P, KEYS], F16)
    pers.wk_h = sc.sb("wk_h", [P, HEADS, 2, DH], F16)
    pers.wk_l = sc.sb("wk_l", [P, HEADS, 2, DH], F16)
    pers.wq_h = sc.sb("wq_h", [P, HEADS, 2, DH], F16)
    pers.wq_l = sc.sb("wq_l", [P, HEADS, 2, DH], F16)
    pers.wv_h = sc.sb("wv_h", [P, HEADS * DH], F16)
    pers.wv_l = sc.sb("wv_l", [P, HEADS * DH], F16)
    pers.att = sc.sb("att", [P, TOKEN_TILES, HEADS * DH])


def build(nc, a, out):
    attention = dict(x=a["x"], ctx=a["ctx_1024"], ln_m_g=a["L0_xattn_ln_m_g"], ln_m_b=a["L0_xattn_ln_m_b"],
                     ln_l_g=a["L0_xattn_ln_l_g"], ln_l_b=a["L0_xattn_ln_l_b"], wq=a["L0_xattn_Wq"],
                     wkv=a["L0_xattn_Wkv"], wout=a["L0_xattn_Wout"])
    experts0 = dict(control=a["L0_ffn_controller"], up=a["L0_ffn_f1"], up_bias=a["L0_ffn_bias"], down=a["L0_ffn_f2"])
    cross = dict(ctx=a["ctx_1024"], w_cq=a["L1_xattn_w_cq"], b_cq=a["L1_xattn_b_cq"], w_c=a["L1_xattn_w_c"],
                 b_c=a["L1_xattn_b_c"], w_q=a["L1_xattn_w_q"], b_q=a["L1_xattn_b_q"], w_l=a["L1_xattn_W_l"],
                 b_l=a["L1_xattn_b_l"])
    experts1 = dict(control=a["L1_ffn_Wc"], control_bias=a["L1_ffn_bc"], up=a["L1_ffn_W1"], up_bias=a["L1_ffn_b1"],
                    down=a["L1_ffn_W2"], down_bias=a["L1_ffn_b2"])
    whole = Scope(nc, "all")
    with whole:
        pers = Persistent(whole)
        shared = Scope(nc, "shared")
        with shared:
            for_attention(pers, shared)
            stage_prepare(nc, pers, attention)
            stage_attention(nc, pers, attention)
            stage_attention_out(nc, pers, attention)
        whole.clear_semaphores()
        later = Scope(nc, "later", whole)
        with later:
            for_later_stages(pers, later)
            ahead = dict(ctx=cross["ctx"], up=experts1["up"], down=experts1["down"])
            stage_experts(nc, pers, experts0, "experts0", 0, ahead=ahead)
            stage_cross(nc, pers, cross)
            stage_experts(nc, pers, experts1, "experts1", 1, out)


_INS = ["x", "ctx_1024", "L0_xattn_ln_m_g", "L0_xattn_ln_m_b", "L0_xattn_ln_l_g", "L0_xattn_ln_l_b", "L0_xattn_Wq",
        "L0_xattn_Wkv", "L0_xattn_Wout", "L0_ffn_controller", "L0_ffn_f1", "L0_ffn_bias", "L0_ffn_f2",
        "L1_xattn_w_cq", "L1_xattn_b_cq", "L1_xattn_w_c", "L1_xattn_b_c", "L1_xattn_w_q", "L1_xattn_b_q",
        "L1_xattn_W_l", "L1_xattn_b_l", "L1_ffn_Wc", "L1_ffn_bc", "L1_ffn_W1", "L1_ffn_b1", "L1_ffn_W2", "L1_ffn_b2"]


def kernel(**inputs):
    import numpy as _np
    import concourse.bacc as _bacc
    from concourse import mybir as _mybir
    from concourse.bass_utils import run_bass_kernel_spmd as _run

    nc = _bacc.Bacc("TRN2", target_bir_lowering=False, num_devices=1)
    arrays, args = {}, {}
    for name in _INS:
        a = _np.ascontiguousarray(inputs[name])
        if a.ndim == 0:
            a = a.reshape(1)
        arrays[f"in_{name}"] = a
        args[name] = nc.dram_tensor(f"in_{name}", a.shape, _mybir.dt.from_np(a.dtype), kind="ExternalInput").ap()
    out = nc.dram_tensor("out", (1, TOKENS, D), F32, kind="ExternalOutput").ap()
    build(nc, args, out)
    r = _run(nc, [arrays], core_ids=[0])
    return r.results[0]["out"]
```
